# Optimizing a Trainium2 kernel written in Bass

```python
import numpy as np
import jax
import jax.numpy as jnp

def _softmax(x, axis=-1):
    return jax.nn.softmax(x, axis=axis)

def _gelu(x):
    return jax.nn.gelu(x, approximate=True)

def _silu(x):
    return jax.nn.silu(x)

def _sigmoid(x):
    return jax.nn.sigmoid(x)

def _layernorm(x, axis=-1, eps=1e-05):
    m = jnp.mean(x, axis=axis, keepdims=True)
    v = jnp.var(x, axis=axis, keepdims=True)
    return (x - m) / jnp.sqrt(v + eps)

def _scatter_add(tgt, idx, src, axis=0):
    return tgt.at[idx].add(src)

def _segment_sum(src, seg, n):
    return jax.ops.segment_sum(src, seg, n)
kernel_name = 'mk_gps_d1_gnn_r8_54e721'

def setup_inputs(seed: int=0):
    np.random.seed(seed)
    _w = jnp.asarray

    def _rec_inputs():
        import jax
        import jax.numpy as jnp
        _gk = jax.random.key(seed)
        x = -8.776e-05 + 1 * jax.random.normal(jax.random.fold_in(_gk, 1), (6250, 256), jnp.float32)
        src = jax.random.randint(jax.random.fold_in(_gk, 2), (100000,), 0, 6250, jnp.int32)
        dst = jax.random.randint(jax.random.fold_in(_gk, 3), (100000,), 0, 6250, jnp.int32)
        _o = jnp.argsort(dst, stable=True)
        src = src[_o]
        dst = dst[_o]
        return (x, src, dst)
    x, src, dst = _rec_inputs()

    def _L0_gnn_setup():
        import jax, jax.numpy as jnp
        import numpy as np
        N = 2500
        E = 40000
        HID = 256
        H = 4
        D = HID // H
        FF = 4 * HID

        def _layernorm(x, g, b, eps=1e-05):
            mu = jnp.mean(x, axis=-1, keepdims=True)
            var = jnp.var(x, axis=-1, keepdims=True)
            return (x - mu) * jax.lax.rsqrt(var + eps) * g + b

        def _transformer_conv(x, edge_index, Wq, bq, Wk, bk, Wv, bv, Wskip, bskip):
            src, dst = (edge_index[0], edge_index[1])
            n = x.shape[0]
            q = (x @ Wq + bq).reshape(n, H, D)
            k = (x @ Wk + bk).reshape(n, H, D)
            v = (x @ Wv + bv).reshape(n, H, D)
            qi = q[dst]
            kj = k[src]
            vj = v[src]
            alpha = jnp.sum(qi * kj, axis=-1) / jnp.sqrt(jnp.float32(D))
            m = jax.ops.segment_max(alpha, dst, num_segments=n)
            ex = jnp.exp(alpha - m[dst])
            denom = jax.ops.segment_sum(ex, dst, num_segments=n)
            a = ex / (denom[dst] + 1e-16)
            out = jax.ops.segment_sum(a[..., None] * vj, dst, num_segments=n)
            out = out.reshape(n, H * D)
            return out + x @ Wskip + bskip
        key = jax.random.key(seed)
        ks = jax.random.split(key, 20)
        w = lambda i, sh: jax.random.normal(ks[i], sh, dtype=jnp.float32) * 0.02
        return {'x': jax.random.normal(ks[0], (N, HID), dtype=jnp.float32), 'edge_index': jax.random.randint(ks[1], (2, E), 0, N, dtype=jnp.int64), 'Wq': w(2, (HID, HID)), 'bq': jnp.zeros((HID,), jnp.float32), 'Wk': w(3, (HID, HID)), 'bk': jnp.zeros((HID,), jnp.float32), 'Wv': w(4, (HID, HID)), 'bv': jnp.zeros((HID,), jnp.float32), 'Wskip': w(5, (HID, HID)), 'bskip': jnp.zeros((HID,), jnp.float32), 'ln1_g': jnp.ones((HID,), jnp.float32), 'ln1_b': jnp.zeros((HID,), jnp.float32), 'W1': w(6, (HID, FF)), 'b1': jnp.zeros((FF,), jnp.float32), 'W2': w(7, (FF, HID)), 'b2': jnp.zeros((HID,), jnp.float32), 'ln2_g': jnp.ones((HID,), jnp.float32), 'ln2_b': jnp.zeros((HID,), jnp.float32)}
    _L0_gnn_all = _L0_gnn_setup()
    _L0_gnn_in = {k: v for k, v in _L0_gnn_all.items() if k in ('Wq', 'bq', 'Wk', 'bk', 'Wv', 'bv', 'Wskip', 'bskip', 'ln1_g', 'ln1_b', 'W1', 'b1', 'W2', 'b2', 'ln2_g', 'ln2_b')}
    del _L0_gnn_all

    def _L0_mix_setup():
        import jax, jax.numpy as jnp
        import numpy as np
        HEADS = 8
        DIM_HEAD = 32
        SCALE = DIM_HEAD ** (-0.5)
        EPS = 1e-05

        def _layernorm_gamma(x, gamma):
            mu = jnp.mean(x, axis=-1, keepdims=True)
            var = jnp.var(x, axis=-1, keepdims=True)
            return (x - mu) * jax.lax.rsqrt(var + EPS) * gamma
        key = jax.random.key(seed)
        k1, k2, k3 = jax.random.split(key, 3)
        B, N, D = (8, 2048, 256)
        hidden = HEADS * DIM_HEAD
        x = jax.random.normal(k1, (B, N, D), dtype=jnp.float32)
        Wqkv = jax.random.normal(k2, (D, 3 * hidden), dtype=jnp.float32) * D ** (-0.5)
        Wout = jax.random.normal(k3, (hidden, D), dtype=jnp.float32) * hidden ** (-0.5)
        gamma = jnp.ones((D,), dtype=jnp.float32)
        return {'x': x, 'Wqkv': Wqkv, 'Wout': Wout, 'gamma': gamma}
    _L0_mix_all = _L0_mix_setup()
    _L0_mix_in = {k: v for k, v in _L0_mix_all.items() if k in ('Wqkv', 'Wout', 'gamma')}
    del _L0_mix_all

    def _L0_ffn_setup():
        import jax, jax.numpy as jnp
        import numpy as np
        NUM_EXPERTS = 8
        TOP_K = 2
        B, S, D = (8, 1024, 256)

        def _moe(tokens, router_w, w1, b1, w2, b2):
            N = tokens.shape[0]
            E = router_w.shape[0]
            logits = tokens.astype(jnp.float32) @ router_w.astype(jnp.float32).T
            probs = jax.nn.softmax(logits, axis=-1)
            rw, re = jax.lax.top_k(probs, TOP_K)
            if TOP_K > 1:
                rw = rw / jnp.maximum(rw.sum(-1, keepdims=True), 1e-12)
            rw = rw.astype(tokens.dtype)
            combine = jnp.zeros((N, E), tokens.dtype).at[jnp.arange(N)[:, None], re].set(rw)
            out = tokens
            for e in range(E):
                h = jax.nn.gelu(tokens @ w1[e] + b1[e], approximate=False)
                y = h @ w2[e] + b2[e]
                out = out + combine[:, e:e + 1] * y
            return out
        key = jax.random.key(seed)
        ks = jax.random.split(key, 4)
        scale = 1.0 / np.sqrt(D).astype(np.float32)
        return {'input_embeddings': jax.random.normal(ks[0], (B, S, D), jnp.float32), 'router_w': jax.random.normal(ks[1], (NUM_EXPERTS, D), jnp.float32) * scale, 'w1': jax.random.normal(ks[2], (NUM_EXPERTS, D, D), jnp.float32) * scale, 'b1': jnp.zeros((NUM_EXPERTS, D), jnp.float32), 'w2': jax.random.normal(ks[3], (NUM_EXPERTS, D, D), jnp.float32) * scale, 'b2': jnp.zeros((NUM_EXPERTS, D), jnp.float32)}
    _L0_ffn_all = _L0_ffn_setup()
    _L0_ffn_in = {k: v for k, v in _L0_ffn_all.items() if k in ('router_w', 'w1', 'b1', 'w2', 'b2')}
    del _L0_ffn_all
    return {'x': x, 'src': src, 'dst': dst, 'L0_gnn_Wq': _L0_gnn_in['Wq'], 'L0_gnn_bq': _L0_gnn_in['bq'], 'L0_gnn_Wk': _L0_gnn_in['Wk'], 'L0_gnn_bk': _L0_gnn_in['bk'], 'L0_gnn_Wv': _L0_gnn_in['Wv'], 'L0_gnn_bv': _L0_gnn_in['bv'], 'L0_gnn_Wskip': _L0_gnn_in['Wskip'], 'L0_gnn_bskip': _L0_gnn_in['bskip'], 'L0_gnn_ln1_g': _L0_gnn_in['ln1_g'], 'L0_gnn_ln1_b': _L0_gnn_in['ln1_b'], 'L0_gnn_W1': _L0_gnn_in['W1'], 'L0_gnn_b1': _L0_gnn_in['b1'], 'L0_gnn_W2': _L0_gnn_in['W2'], 'L0_gnn_b2': _L0_gnn_in['b2'], 'L0_gnn_ln2_g': _L0_gnn_in['ln2_g'], 'L0_gnn_ln2_b': _L0_gnn_in['ln2_b'], 'L0_mix_Wqkv': _L0_mix_in['Wqkv'], 'L0_mix_Wout': _L0_mix_in['Wout'], 'L0_mix_gamma': _L0_mix_in['gamma'], 'L0_ffn_router_w': _L0_ffn_in['router_w'], 'L0_ffn_w1': _L0_ffn_in['w1'], 'L0_ffn_b1': _L0_ffn_in['b1'], 'L0_ffn_w2': _L0_ffn_in['w2'], 'L0_ffn_b2': _L0_ffn_in['b2']}

def reference(x, src, dst, L0_gnn_Wq, L0_gnn_bq, L0_gnn_Wk, L0_gnn_bk, L0_gnn_Wv, L0_gnn_bv, L0_gnn_Wskip, L0_gnn_bskip, L0_gnn_ln1_g, L0_gnn_ln1_b, L0_gnn_W1, L0_gnn_b1, L0_gnn_W2, L0_gnn_b2, L0_gnn_ln2_g, L0_gnn_ln2_b, L0_mix_Wqkv, L0_mix_Wout, L0_mix_gamma, L0_ffn_router_w, L0_ffn_w1, L0_ffn_b1, L0_ffn_w2, L0_ffn_b2):
    import jax
    import jax.numpy as jnp

    def _L0_gnn_ref(x, edge_index, Wq, bq, Wk, bk, Wv, bv, Wskip, bskip, ln1_g, ln1_b, W1, b1, W2, b2, ln2_g, ln2_b):
        import jax, jax.numpy as jnp
        import numpy as np
        N = 2500
        E = 40000
        HID = 256
        H = 4
        D = HID // H
        FF = 4 * HID

        def _layernorm(x, g, b, eps=1e-05):
            mu = jnp.mean(x, axis=-1, keepdims=True)
            var = jnp.var(x, axis=-1, keepdims=True)
            return (x - mu) * jax.lax.rsqrt(var + eps) * g + b

        def _transformer_conv(x, edge_index, Wq, bq, Wk, bk, Wv, bv, Wskip, bskip):
            src, dst = (edge_index[0], edge_index[1])
            n = x.shape[0]
            q = (x @ Wq + bq).reshape(n, H, D)
            k = (x @ Wk + bk).reshape(n, H, D)
            v = (x @ Wv + bv).reshape(n, H, D)
            qi = q[dst]
            kj = k[src]
            vj = v[src]
            alpha = jnp.sum(qi * kj, axis=-1) / jnp.sqrt(jnp.float32(D))
            m = jax.ops.segment_max(alpha, dst, num_segments=n)
            ex = jnp.exp(alpha - m[dst])
            denom = jax.ops.segment_sum(ex, dst, num_segments=n)
            a = ex / (denom[dst] + 1e-16)
            out = jax.ops.segment_sum(a[..., None] * vj, dst, num_segments=n)
            out = out.reshape(n, H * D)
            return out + x @ Wskip + bskip
        x_new = _transformer_conv(x, edge_index, Wq, bq, Wk, bk, Wv, bv, Wskip, bskip)
        h = _layernorm(x + x_new, ln1_g, ln1_b)
        ffn = jax.nn.gelu(h @ W1 + b1, approximate=False) @ W2 + b2
        return _layernorm(h + ffn, ln2_g, ln2_b)

    def _L0_mix_ref(x, Wqkv, Wout, gamma):
        import jax, jax.numpy as jnp
        import numpy as np
        HEADS = 8
        DIM_HEAD = 32
        SCALE = DIM_HEAD ** (-0.5)
        EPS = 1e-05

        def _layernorm_gamma(x, gamma):
            mu = jnp.mean(x, axis=-1, keepdims=True)
            var = jnp.var(x, axis=-1, keepdims=True)
            return (x - mu) * jax.lax.rsqrt(var + EPS) * gamma
        B, N, D = x.shape
        qkv = x @ Wqkv
        q, k, v = jnp.split(qkv, 3, axis=-1)

        def to_heads(t):
            return t.reshape(B, N, HEADS, DIM_HEAD).transpose(0, 2, 1, 3)
        q, k, v = map(to_heads, (q, k, v))
        q = jax.nn.softmax(q, axis=-1) * SCALE
        k = jax.nn.softmax(k, axis=2)
        context = jnp.einsum('bhnd,bhne->bhde', k, v)
        out = jnp.einsum('bhde,bhnd->bhne', context, q)
        out = out.transpose(0, 2, 1, 3).reshape(B, N, HEADS * DIM_HEAD)
        out = out @ Wout
        return _layernorm_gamma(out, gamma)

    def _L0_ffn_ref(input_embeddings, router_w, w1, b1, w2, b2):
        import jax, jax.numpy as jnp
        import numpy as np
        NUM_EXPERTS = 8
        TOP_K = 2
        B, S, D = (8, 1024, 256)

        def _moe(tokens, router_w, w1, b1, w2, b2):
            N = tokens.shape[0]
            E = router_w.shape[0]
            logits = tokens.astype(jnp.float32) @ router_w.astype(jnp.float32).T
            probs = jax.nn.softmax(logits, axis=-1)
            rw, re = jax.lax.top_k(probs, TOP_K)
            if TOP_K > 1:
                rw = rw / jnp.maximum(rw.sum(-1, keepdims=True), 1e-12)
            rw = rw.astype(tokens.dtype)
            combine = jnp.zeros((N, E), tokens.dtype).at[jnp.arange(N)[:, None], re].set(rw)
            out = tokens
            for e in range(E):
                h = jax.nn.gelu(tokens @ w1[e] + b1[e], approximate=False)
                y = h @ w2[e] + b2[e]
                out = out + combine[:, e:e + 1] * y
            return out
        b, s, d = input_embeddings.shape
        tokens = input_embeddings.reshape(b * s, d)
        return _moe(tokens, router_w, w1, b1, w2, b2).reshape(b, s, d)
    edge_index = jnp.stack([src, dst])
    xn = _layernorm(x, axis=-1)
    x = x + _L0_gnn_ref(xn, edge_index, L0_gnn_Wq, L0_gnn_bq, L0_gnn_Wk, L0_gnn_bk, L0_gnn_Wv, L0_gnn_bv, L0_gnn_Wskip, L0_gnn_bskip, L0_gnn_ln1_g, L0_gnn_ln1_b, L0_gnn_W1, L0_gnn_b1, L0_gnn_W2, L0_gnn_b2, L0_gnn_ln2_g, L0_gnn_ln2_b) + _L0_mix_ref(xn[None], L0_mix_Wqkv, L0_mix_Wout, L0_mix_gamma)[0]
    x = x + _L0_ffn_ref(_layernorm(x, axis=-1)[None], L0_ffn_router_w, L0_ffn_w1, L0_ffn_b1, L0_ffn_w2, L0_ffn_b2)[0]
    return x

_drawn_inputs = setup_inputs


def setup_inputs(seed=0):
    import zlib

    import numpy as np

    out = dict(_drawn_inputs(seed))
    spreads = {'L0_gnn_bq': (0.0, 0.8),
     'L0_gnn_bk': (0.0, 0.8),
     'L0_gnn_bv': (0.0, 0.1),
     'L0_gnn_bskip': (0.0, 0.1),
     'L0_gnn_ln1_g': (1.0, 0.2),
     'L0_gnn_ln1_b': (0.0, 0.1),
     'L0_gnn_b1': (0.0, 0.365),
     'L0_gnn_b2': (0.0, 0.1),
     'L0_gnn_ln2_g': (1.0, 0.2),
     'L0_gnn_ln2_b': (0.0, 0.1),
     'L0_mix_gamma': (1.0, 0.2),
     'L0_ffn_b1': (0.0, 0.494),
     'L0_ffn_b2': (0.0, 0.339)}
    factors = {'L0_gnn_Wq': 7.232, 'L0_gnn_Wk': 6.975}
    for name, (base, spread) in spreads.items():
        noise = np.random.default_rng([zlib.crc32(name.encode()), seed]).standard_normal(out[name].shape)
        drawn = base * np.exp(spread * noise) if base else spread * noise
        out[name] = jnp.asarray(drawn.astype(out[name].dtype))
    for name, factor in factors.items():
        out[name] = (out[name] * factor).astype(out[name].dtype)
    return out
```

```python
import concourse.bass as bass
from concourse import mybir
from contextlib import ExitStack

F32 = mybir.dt.float32
BF16 = mybir.dt.bfloat16
I32 = mybir.dt.int32
U32 = mybir.dt.uint32
ALU = mybir.AluOpType
ACT = mybir.ActivationFunctionType
AX = mybir.AxisListType.X

N, D = 6250, 256
E = 100000
P = 125
NT = N // P
EG = 2 * P
NG = E // EG
H, HD = 4, D // 4
MH, MD = 8, D // 8
FF = 4 * D
NE = 8
KC = D // 128
NF = FF // 128
NGR = NT // 2
ACC_STEPS = NE + 1
HB_BODY = NF + NE * KC
BODY_LINKS = 96
NSMALL = 9 + NE
GC = 4
GP = NG // GC
SPC = 8
NCH = 57
NSTEP = NCH * SPC
T = 2 * SPC
R = H * T
VH = HD + 1
SLOT = H * VH
RING = 3
NEG = -float(2 ** 100)
EPS = 1e-5
MAGIC = 0x5F3759DF


def ds(start, size):
    return bass.ds(start, size)


def wait(eng, sem, value):
    if isinstance(value, int) and value <= 0:
        return
    eng.wait_ge(sem, value)


class Count:

    def __init__(self, eng, sem, at=0):
        self.eng, self.sem, self.at = eng, sem, at

    def mark(self, ins):
        ins.then_inc(self.sem, 1)
        self.at = self.at + 1
        return self.at

    def chain(self, ins):
        self.mark(ins)
        self.eng.wait_ge(self.sem, self.at)


def hold(dve, cell):
    dve.memset(cell, 0.0)


def rsqrt_newton(dve, cnt, var, half, y, t):
    yi, ti = y.bitcast(I32), t.bitcast(I32)
    cnt.chain(dve.tensor_scalar(t, var, EPS, None, ALU.add))
    cnt.mark(dve.tensor_scalar(half, t, -0.5, None, ALU.mult))
    cnt.chain(dve.tensor_scalar(yi, ti, 1, None, ALU.arith_shift_right))
    cnt.chain(dve.tensor_scalar(yi, yi, -1, MAGIC, ALU.mult, ALU.add))
    for _ in range(3):
        cnt.chain(dve.tensor_tensor(t, y, y, ALU.mult))
        cnt.chain(dve.tensor_tensor(t, t, half, ALU.mult))
        cnt.chain(dve.scalar_tensor_tensor(y, t, 1.5, y, ALU.add, ALU.mult))


def constants(nc, c):
    with ExitStack() as ctx:
        s_set = ctx.enter_context(nc.semaphore("const_set"))
        s_zero = ctx.enter_context(nc.semaphore("mask_zeroed"))
        block = ctx.enter_context(nc.Block())

        @block.gpsimd
        def _(pool):
            cnt = Count(pool, s_set)
            cnt.mark(pool.memset(c.ident[:, :], 0.0))
            cnt.mark(pool.iota(c.iota[:, :], pattern=[[1, 128]], base=0, channel_multiplier=0,
                               allow_small_or_imprecise_dtypes=True))
            pool.wait_ge(s_set, cnt.at)
            pool.affine_select(out=c.ident[:, :], in_=c.ident[:, :], compare_op=ALU.not_equal, fill=1.0,
                               base=0, pattern=[[-1, 128]], channel_multiplier=1)

        @block.vector
        def _(dve):
            dve.memset(c.ones[:, :], 1.0)
            dve.memset(c.slots[:, 0, 0:D], 0.0)
            dve.memset(c.slots[:, :, D:SLOT], 0.0)
            dve.memset(c.headmask[:, :], 0.0).then_inc(s_zero, 1)
            dve.wait_ge(s_zero, 1)
            for k in range(128 // MD):
                dve.memset(c.headmask[k * MD:(k + 1) * MD, k * MD:(k + 1) * MD], 1.0)


class Consts:
    def __init__(self, ctx, nc):
        def sb(name, shape, dt=F32):
            return ctx.enter_context(nc.sbuf_tensor(name, shape, dt))
        self.ident = sb("ident", [128, 128])
        self.ones = sb("ones", [128, 128])
        self.headmask = sb("headmask", [128, 128])
        self.iota = sb("iota", [128, 128])
        self.slots = sb("slots", [P, NT + 1, SLOT])
        self.mixmat = sb("mixmat", [128, KC, D])


class Group:

    def __init__(self, k, off):
        self.k, self.off = k, off
        self.i, self.b, self.turn = 2 * k + off, off % 2, k + off // 2

    def plus(self, n):
        return Group(self.k, self.off + n)

    def within(self, low, high):
        return not isinstance(self.i, int) or low <= self.i < high


def group_bodies(eng, body, extra=0):
    for g in range(3):
        body(Group(0, g))
    with eng.Fori(1, (NGR - 3) // 2) as k:
        body(Group(k, 1))
        body(Group(k, 2))
    for g in range(NGR - 2, NGR + extra):
        body(Group((NGR - 3) // 2, g - (NGR - 3)))


def node_phase(nc, c, x, w, kv_d, s1_d, qm_d):
    with ExitStack() as ctx:
        def sb(name, shape, dt=F32):
            return ctx.enter_context(nc.sbuf_tensor("n_" + name, shape, dt))

        def ps(name, shape=(128, 512)):
            return ctx.enter_context(nc.psum_tensor("n_" + name, list(shape), F32))

        def sem(name):
            return ctx.enter_context(nc.semaphore("n_" + name))

        wg = sb("wg", [128, KC, 4 * D])
        wm = sb("wm", [128, KC, 3 * D])
        wo = sb("wo", [128, KC, D])
        bias = sb("bias", [P, 4, D])
        kmix = sb("kmix", [P, NT, D])
        vmix = sb("vmix", [P, NT, KC, 129])
        xt = sb("xt", [P, 2, 2, D])
        xn = sb("xn", [P, 2, 2, D])
        xnb = sb("xnb", [P, 2, D])
        xnT = sb("xnT", [128, 2, KC, P])
        kv = sb("kv", [P, 2, 2 * D])
        s1 = sb("s1", [P, 2, D])
        eq = sb("eq", [P, 2, D])
        qm = sb("qm", [P, 2, D])
        st = sb("st", [P, 2, 6])
        mv = sb("mv", [P, 2, 2])
        rstd = sb("rstd", [P, 2])
        power = sb("power", [P, 2, 2])
        cell = sb("cell", [1, 1])
        hm = sb("hm", [P, 3, MH])
        rmax = sb("rmax", [P, D])
        mcol = sb("mcol", [128, KC])
        mrow = sb("mrow", [1, D])
        mb = sb("mb", [P, D])
        ek = sb("ek", [P, 2, D])
        rz = sb("rz", [128, KC])
        cxn = sb("cxn", [128, KC, 128])
        cxT = sb("cxT", [128, KC, 128])
        pT = ps("pT")
        pqk, pvs, pmqk, pmv = ps("pqk"), ps("pvs"), ps("pmqk"), ps("pmv")
        pcx = [ps(f"pcx{k}") for k in range(KC)]

        s_w = sem("weights_in")
        s_b = sem("biases_in")
        s_x = [sem(f"x_in{b}") for b in range(2)]
        s_st, s_var, s_rstd, s_eps, s_pw = (sem(n) for n in ("stats", "variance", "rstd", "var_eps", "power_set"))
        s_sm = sem("softmax_link")
        s_d = sem("context_link")
        s_xn = sem("xn_made")
        s_xnb = sem("xnb_made")
        s_T = sem("xnT_in_psum")
        s_Tc = sem("xnT_made")
        s_g = [sem(f"proj{g}_made") for g in range(4)]
        s_qk = sem("qk_taken")
        s_vs = sem("vs_taken")
        s_eqr = sem("mixq_shifted")
        s_eq = sem("mixq_exp")
        s_rs = sem("mixq_rsum")
        s_qm = sem("mixq_made")
        s_km = sem("mixk_kept")
        s_vm = sem("mixv_kept")
        s_rm = sem("rmax_made")
        s_kvo = [sem(f"kv_out{b}") for b in range(2)]
        s_s1o = [sem(f"s1_out{b}") for b in range(2)]
        s_qmo = [sem(f"qm_out{b}") for b in range(2)]
        s_one = sem("vones_set")
        s_rT, s_mc, s_mrT, s_mr, s_mbT = (sem(n) for n in ("rmaxT", "mcol", "mrowT", "mrow", "mb_in_psum"))
        s_ks, s_ek, s_cx = sem("key_shifted"), sem("key_exp"), sem("context_added")
        s_cn, s_cT, s_cTc, s_mm, s_end = (sem(n) for n in ("ctx_scaled", "ctxT", "ctxT_kept", "mix_made", "mix_kept"))
        block = ctx.enter_context(nc.Block())

        last_k = NT // 2 - 1

        def tiles(eng, body):
            for b in range(2):
                body(0, b)
            with eng.Fori(1, last_k) as k:
                for b in range(2):
                    body(k, b)
            for b in range(2):
                body(last_k, b)

        @block.sync
        def _(sp):
            for k, name in enumerate(("Wq", "Wk", "Wv", "Wskip")):
                sp.dma_start(wg[:, :, k * D:(k + 1) * D],
                             w["L0_gnn_" + name].rearrange("(c p) n -> p c n", p=128)).then_inc(s_w, 16)
            sp.dma_start(wm[:, :, :], w["L0_mix_Wqkv"].rearrange("(c p) n -> p c n", p=128)).then_inc(s_w, 16)
            sp.dma_start(wo[:, :, :], w["L0_mix_Wout"].rearrange("(c p) n -> p c n", p=128)).then_inc(s_w, 16)

            def load(g):
                wait(sp, s_xn, 2 * (g.i - 1))
                sp.dma_start(xt[:, g.b, :, :],
                             x[ds(g.i * (2 * P), 2 * P), :].rearrange("(t p) d -> p t d", p=P)).then_inc(s_x[g.b], 16)

            def store_qm(n, b):
                sp.wait_ge(s_qm, n + 1)
                sp.dma_start(qm_d[ds(n * P, P), :], qm[:, b, :]).then_inc(s_qmo[b], 16)

            load(Group(0, 0))
            for k, name in enumerate(("bq", "bk", "bv", "bskip")):
                sp.dma_start(bias[:, k, :], w["L0_gnn_" + name].partition_broadcast(P)).then_inc(s_b, 16)
            load(Group(0, 1))

            def body(g):
                if g.within(0, NGR - 2):
                    load(g.plus(2))
                for j in range(2):
                    n = 2 * g.i + j
                    sp.wait_ge(s_qk, n + 1)
                    sp.wait_ge(s_vs, n + 1)
                    sp.dma_start(kv_d[ds(n * P, P), :], kv[:, j, :]).then_inc(s_kvo[j], 16)
                    sp.dma_start(s1_d[ds(n * P, P), :], s1[:, j, :]).then_inc(s_s1o[j], 16)
                    if j or g.within(1, NGR):
                        store_qm(n - 1, 1 - j)

            group_bodies(sp, body)
            store_qm(NT - 1, 1)
            for s in (s_kvo, s_s1o, s_qmo):
                for b in range(2):
                    sp.wait_ge(s[b], 16 * (NT // 2))

        @block.vector
        def _(dve):
            def variance(g):
                dve.wait_ge(s_x[g.b], 16 * g.turn + 16)
                for j in range(2):
                    dve.bn_stats(st[:, j, :], xt[:, g.b, j, :]).then_inc(s_st, 1)
                dve.wait_ge(s_st, 2 * g.i + 2)
                wait(dve, s_xn, 2 * g.i)
                hold(dve, cell[:, :])
                for j in range(2):
                    dve.bn_aggr(mv[:, j, :], st[:, j, :]).then_inc(s_var, 1)

            def normalise(g):
                dve.wait_ge(s_rstd, g.i + 1)
                if g.within(2, NGR):
                    dve.wait_ge(s_xnb, 2 * g.i - 2)
                    dve.wait_ge(s_T, 2 * g.i - 2)
                for j in range(2):
                    dve.tensor_scalar(xn[:, g.b, j, :], xt[:, g.b, j, :], mv[:, j, 0:1], rstd[:, j:j + 1],
                                      ALU.subtract, ALU.mult).then_inc(s_xn, 1)

            def mixq_sum(n, b):
                dve.wait_ge(s_eq, n + 1)
                dve.tensor_reduce(hm[:, 1, :], eq[:, b, :].rearrange("p (h d) -> p h d", h=MH), AX, ALU.add
                                  ).then_inc(s_sm, 1)
                dve.wait_ge(s_sm, 2 * n + 2)
                wait(dve, s_qm, n)
                dve.reciprocal(hm[:, 2, :], hm[:, 1, :]).then_inc(s_rs, 1)

            def tile(g, j):
                n = 2 * g.i + j
                dve.wait_ge(s_g[0], n + 1)
                dve.tensor_tensor(c.slots[:, ds(n + 1, 1), 0:D].rearrange("p a d -> p (a d)"),
                                  pqk[0:P, 0:D], bias[:, 0, :], ALU.add)
                wait(dve, s_kvo[j], 16 * g.i)
                dve.tensor_tensor(kv[:, j, 0:D], pqk[0:P, D:2 * D], bias[:, 1, :], ALU.add).then_inc(s_qk, 1)
                if j or g.within(1, NGR):
                    mixq_sum(n - 1, 1 - j)
                dve.wait_ge(s_g[1], n + 1)
                dve.tensor_tensor(kv[:, j, D:2 * D], pvs[0:P, 0:D], bias[:, 2, :], ALU.add)
                dve.wait_ge(s_xnb, n + 1)
                wait(dve, s_s1o[j], 16 * g.i)
                dve.tensor_tensor(s1[:, j, :], pvs[0:P, D:2 * D], xnb[:, j, :], ALU.add).then_inc(s_vs, 1)
                if j == 0 and g.within(0, NGR - 1):
                    variance(g.plus(1))
                dve.wait_ge(s_g[2], n + 1)
                q3 = pmqk[0:P, 0:D].rearrange("p (h d) -> p h d", h=MH)
                dve.tensor_reduce(hm[:, 0, :], q3, AX, ALU.max).then_inc(s_sm, 1)
                if j == 0 and not g.within(1, NGR):
                    dve.tensor_copy(rmax[:, :], pmqk[0:P, D:2 * D]).then_inc(s_rm, 1)
                else:
                    dve.wait_ge(s_rm, n)
                    dve.tensor_tensor(rmax[:, :], rmax[:, :], pmqk[0:P, D:2 * D], ALU.max).then_inc(s_rm, 1)
                dve.wait_ge(s_sm, 2 * n + 1)
                wait(dve, s_qm, n - 1)
                dve.tensor_tensor(eq[:, j, :].rearrange("p (h d) -> p h d", h=MH), q3,
                                  hm[:, 0, :].unsqueeze(2).broadcast_to([P, MH, MD]), ALU.subtract).then_inc(s_eqr, 1)
                if j == 0 and g.within(0, NGR - 1):
                    normalise(g.plus(1))

            variance(Group(0, 0))
            normalise(Group(0, 0))
            dve.wait_ge(s_b, 64)

            def body(g):
                for j in range(2):
                    tile(g, j)

            group_bodies(dve, body)
            mixq_sum(NT - 1, 1)

            cnt = Count(dve, s_d)
            dve.wait_ge(s_rT, 1)
            dve.tensor_reduce(mcol[:, :], pT[:, 0:2 * P].rearrange("p (c n) -> p c n", c=KC),
                              AX, ALU.max).then_inc(s_mc, 1)
            dve.wait_ge(s_mrT, 1)
            dve.tensor_copy(mrow[:, :], pmv[0:1, 0:D]).then_inc(s_mr, 1)
            dve.wait_ge(s_mbT, 1)
            cnt.chain(dve.tensor_copy(mb[:, :], pvs[0:P, 0:D]))

            def shift(k, b):
                n = 2 * k + b
                wait(dve, s_cx, n - 1 if not isinstance(k, int) or k else 0)
                dve.tensor_tensor(ek[:, b, :], kmix[:, ds(n, 1), :].rearrange("p a d -> p (a d)"), mb[:, :],
                                  ALU.subtract).then_inc(s_ks, 1)

            tiles(dve, shift)
            dve.wait_ge(s_cx, NT)
            for cc in range(KC):
                cnt.chain(dve.reciprocal(rz[:, cc:cc + 1], pcx[cc][:, 128:129]))
                cnt.chain(dve.tensor_scalar(cxn[:, cc, :], pcx[cc][:, 0:128], rz[:, cc:cc + 1], MD ** -0.5,
                                            ALU.mult, ALU.mult))
                dve.tensor_tensor(cxn[:, cc, :], cxn[:, cc, :], c.headmask[:, :], ALU.mult).then_inc(s_cn, 1)
            dve.wait_ge(s_cT, 1)
            dve.tensor_copy(cxT[:, :, :], pT[:, 0:256].rearrange("p (c n) -> p c n", c=KC)).then_inc(s_cTc, 1)
            dve.wait_ge(s_mm, 1)
            dve.tensor_copy(c.mixmat[:, :, :], pqk[:, :].rearrange("p (c n) -> p c n", c=KC)).then_inc(s_end, 1)

        @block.gpsimd
        def _(pool):
            pool.memset(power[:, 0, :], -0.5).then_inc(s_pw, 1)
            pool.memset(power[:, 1, :], EPS).then_inc(s_pw, 1)
            pool.memset(vmix[:, :, :, 128:129], 1.0).then_inc(s_one, 1)
            pool.wait_ge(s_pw, 2)
            pool.wait_ge(s_b, 64)

            def reciprocal_root(g):
                pool.wait_ge(s_var, 2 * g.i + 2)
                wait(pool, s_xn, 2 * g.i)
                pool.tensor_tensor(rstd[:, :], mv[:, :, 1], power[:, 1, :], ALU.add).then_inc(s_eps, 1)
                pool.wait_ge(s_eps, g.i + 1)
                pool.tensor_tensor(rstd[:, :], rstd[:, :], power[:, 0, :], ALU.pow).then_inc(s_rstd, 1)

            def with_bias(g, j):
                n = 2 * g.i + j
                pool.wait_ge(s_xn, n + 1)
                wait(pool, s_vs, n - 1)
                pool.tensor_tensor(xnb[:, j, :], xn[:, g.b, j, :], bias[:, 3, :], ALU.add).then_inc(s_xnb, 1)

            def mixq(n, j, turn):
                pool.wait_ge(s_rs, n + 1)
                wait(pool, s_qmo[j], 16 * turn)
                pool.tensor_tensor(qm[:, j, :].rearrange("p (h d) -> p h d", h=MH),
                                   eq[:, j, :].rearrange("p (h d) -> p h d", h=MH),
                                   hm[:, 2, :].unsqueeze(2).broadcast_to([P, MH, MD]), ALU.mult).then_inc(s_qm, 1)

            def body(g):
                if g.within(1, NGR):
                    mixq(2 * g.i - 1, 1, g.i - 1)
                with_bias(g, 1)
                if g.within(0, NGR - 1):
                    reciprocal_root(g.plus(1))
                mixq(2 * g.i, 0, g.i)
                if g.within(0, NGR - 1):
                    with_bias(g.plus(1), 0)

            reciprocal_root(Group(0, 0))
            pool.wait_ge(s_b, 64)
            with_bias(Group(0, 0), 0)
            group_bodies(pool, body)
            mixq(NT - 1, 1, NGR - 1)

        @block.scalar
        def _(act):
            def keep_turned(n, b):
                act.wait_ge(s_T, n + 1)
                wait(act, s_g[3], n - 1)
                act.activation(xnT[:, b, :, :], pT[:, 0:2 * P].rearrange("p (c n) -> p c n", c=KC),
                               ACT.Copy).then_inc(s_Tc, 1)

            def body(g):
                for j in range(2):
                    n = 2 * g.i + j
                    if j == 0 or g.within(0, NGR - 1):
                        keep_turned(n + 1, 1 - j)
                    act.wait_ge(s_eqr, n + 1)
                    act.activation(kmix[:, ds(n, 1), :].rearrange("p a d -> p (a d)"), pmqk[0:P, D:2 * D],
                                   ACT.Copy).then_inc(s_km, 1)
                    act.activation(eq[:, j, :], eq[:, j, :], ACT.Exp).then_inc(s_eq, 1)
                    act.wait_ge(s_g[3], n + 1)
                    act.activation(vmix[:, ds(n, 1), :, 0:128].rearrange("p a c d -> p (a c) d"),
                                   pmv[0:P, 0:D].rearrange("p (c d) -> p c d", c=KC), ACT.Copy).then_inc(s_vm, 1)

            keep_turned(0, 0)
            group_bodies(act, body)

            def keyexp(k, b):
                act.wait_ge(s_ks, 2 * k + b + 1)
                act.activation(ek[:, b, :], ek[:, b, :], ACT.Exp).then_inc(s_ek, 1)

            tiles(act, keyexp)

        @block.tensor
        def _(pe):
            def turn(g, j):
                n = 2 * g.i + j
                pe.wait_ge(s_xn, n + 1)
                wait(pe, s_Tc, n)
                for cc in range(KC):
                    t = pe.transpose(pT[:, cc * P:(cc + 1) * P], xn[:, g.b, j, cc * 128:(cc + 1) * 128],
                                     c.ident[0:P, 0:P])
                t.then_inc(s_T, 1)

            def project(n, b, g, out, weights, freed):
                for s in freed:
                    wait(pe, s, n)
                for cc in range(KC):
                    m = pe.matmul(out, xnT[:, b, cc, :], weights(cc), start=cc == 0, stop=cc == KC - 1)
                m.then_inc(s_g[g], 1)

            def body(g):
                for j in range(2):
                    n = 2 * g.i + j
                    pe.wait_ge(s_Tc, n + 1)
                    project(n, j, 0, pqk[0:P, :], lambda cc: wg[:, cc, 0:2 * D], [s_qk])
                    project(n, j, 1, pvs[0:P, :], lambda cc: wg[:, cc, 2 * D:4 * D], [s_vs])
                    if j == 0 or g.within(0, NGR - 1):
                        turn(g.plus(j), 1 - j)
                    project(n, j, 2, pmqk[0:P, :], lambda cc: wm[:, cc, 0:2 * D], [s_km])
                    project(n, j, 3, pmv[0:P, 0:D], lambda cc: wm[:, cc, 2 * D:3 * D], [s_vm])

            turn(Group(0, 0), 0)
            pe.wait_ge(s_w, 16 * 6)
            group_bodies(pe, body)

            pe.wait_ge(s_rm, NT)
            pe.wait_ge(s_Tc, NT)
            for cc in range(KC):
                t = pe.transpose(pT[:, cc * P:(cc + 1) * P], rmax[:, cc * 128:(cc + 1) * 128], c.ident[0:P, 0:P])
            t.then_inc(s_rT, 1)
            pe.wait_ge(s_mc, 1)
            pe.wait_ge(s_vm, NT)
            for cc in range(KC):
                t = pe.transpose(pmv[0:1, cc * 128:(cc + 1) * 128], mcol[:, cc:cc + 1], c.ident[:, :])
            t.then_inc(s_mrT, 1)
            pe.wait_ge(s_mr, 1)
            pe.wait_ge(s_vs, NT)
            pe.matmul(pvs[0:P, 0:D], c.ones[0:1, 0:P], mrow[:, :], start=True, stop=True).then_inc(s_mbT, 1)
            pe.wait_ge(s_one, 1)

            def context(k, b):
                n = 2 * k + b
                pe.wait_ge(s_ek, n + 1)
                for cc in range(KC):
                    m = pe.matmul(pcx[cc][:, 0:129], ek[:, b, cc * 128:(cc + 1) * 128],
                                  vmix[:, ds(n, 1), cc, :].rearrange("p a d -> p (a d)"),
                                  start=isinstance(k, int) and n == 0, stop=isinstance(k, int) and n == NT - 1)
                m.then_inc(s_cx, 1)

            tiles(pe, context)
            pe.wait_ge(s_cn, KC)
            for cc in range(KC):
                t = pe.transpose(pT[:, cc * 128:(cc + 1) * 128], cxn[:, cc, :], c.ident[:, :])
            t.then_inc(s_cT, 1)
            pe.wait_ge(s_cTc, 1)
            for cc in range(KC):
                m = pe.matmul(pqk[:, cc * D:(cc + 1) * D], cxT[:, cc, :], wo[:, cc, :], start=True, stop=True)
            m.then_inc(s_mm, 1)


class Chunk:

    def __init__(self, i, off):
        self.i, self.off = i, off
        self.c, self.ring, self.turn = RING * i + off, off % RING, i + off // RING

    def plus(self, k):
        return Chunk(self.i, self.off + k)

    def within(self, low, high):
        return not isinstance(self.c, int) or low <= self.c < high

    def step(self, s):
        k = self.plus(s // SPC)
        return (k, s % SPC) if k.within(0, NCH) else None


def chunk_bodies(eng, body):
    for c in range(-1, RING):
        body(Chunk(0, c))
    with eng.Fori(1, NCH // RING - 1) as i:
        for u in range(RING):
            body(Chunk(i, u))
    for c in range(NCH - RING, NCH + 2):
        body(Chunk(NCH // RING - 1, c - (NCH - RING)))


class Steps:

    def __init__(self, ctx, nc):
        def sb(name, shape, dt=F32):
            return ctx.enter_context(nc.sbuf_tensor("e_" + name, shape, dt))
        self.src = sb("src", [P, 2 * NSTEP], I32)
        self.row = sb("row", [P, 2 * NSTEP])
        self.breaks = sb("breaks", [P, 2, 2 * NSTEP], BF16)
        self.mask = sb("mask", [P, 2 * NSTEP], BF16)
        self.keep = sb("keep", [P, NSTEP])
        self.tile = sb("tile", [1, NSTEP], I32)


def step_tables(nc, c, st, src, dst):
    with ExitStack() as ctx:
        def sb(name, shape, dt=F32):
            return ctx.enter_context(nc.sbuf_tensor("t_" + name, shape, dt))

        def sem(name):
            return ctx.enter_context(nc.semaphore("t_" + name))

        raw = sb("raw", [GP, 4, GC, EG], I32)
        val = sb("val", [GP, 4, GC, EG])
        thr = sb("thr", [GP, NT - 1])
        steps = sb("steps", [128, NSTEP])
        le = sb("le", [GP, GC, NT - 1])
        gid = sb("gid", [GP, GC])
        last = sb("last", [GP, GC])
        past = sb("past", [GP, GC, NSTEP])
        gq = sb("gq", [128, NSTEP])
        nq = sb("nq", [128, NSTEP])
        pick = sb("pick", [GP, GC, NSTEP])
        m2 = sb("m2", [P, 2, 2 * NSTEP])
        ps = [ctx.enter_context(nc.psum_tensor(f"t_ps{k}", [128, 512], F32)) for k in range(8)]
        s_set, s_in, s_io = sem("set"), sem("in"), sem("iota")
        s_v, s_past, s_cnt, s_pick, s_got = sem("link"), sem("past"), sem("cnt"), sem("pick"), sem("got")
        block = ctx.enter_context(nc.Block())

        @block.gpsimd
        def _(pool):
            pool.iota(gid[:, :], pattern=[[GP, GC]], base=0, channel_multiplier=1,
                      allow_small_or_imprecise_dtypes=True).then_inc(s_io, 1)
            pool.iota(steps[:, :], pattern=[[1, NSTEP]], base=0, channel_multiplier=0,
                      allow_small_or_imprecise_dtypes=True).then_inc(s_io, 1)
            pool.iota(thr[:, :], pattern=[[P, NT - 1]], base=P, channel_multiplier=0,
                      allow_small_or_imprecise_dtypes=True).then_inc(s_io, 1)

        @block.sync
        def _(sp):
            groups = dst.rearrange("(c g e) -> g c e", g=GP, e=EG)
            rows = dst.rearrange("(g e) -> g e", e=EG)
            sp.dma_start(raw[:, 0, :, :], groups).then_inc(s_in, 16)
            sp.dma_start(raw[:, 1, :, :], src.rearrange("(c g e) -> g c e", g=GP, e=EG)).then_inc(s_in, 16)
            sp.wait_ge(s_set, 1)
            with nc.allow_non_contiguous_dma("one element of each group"):
                for cc in range(GC):
                    sp.dma_start(raw[:, 2, cc, 1:EG], groups[:, cc, 0:EG - 1]).then_inc(s_in, 16)
                    sp.dma_start(raw[:, 3, cc, 0:EG - 1], groups[:, cc, 1:EG]).then_inc(s_in, 16)
                    lo = 1 if cc == 0 else 0
                    hi = GP - 1 if cc == GC - 1 else GP
                    sp.dma_start(raw[lo:GP, 2, cc, 0:1], rows[cc * GP + lo - 1:cc * GP + GP - 1, EG - 1:EG]).then_inc(s_in, 16)
                    sp.dma_start(raw[0:hi, 3, cc, EG - 1:EG], rows[cc * GP + 1:cc * GP + hi + 1, 0:1]).then_inc(s_in, 16)

        @block.vector
        def _(dve):
            cnt = Count(dve, s_v)
            dve.memset(raw[0:1, 2, 0, 0:1], -1)
            dve.memset(raw[96:GP, 3, GC - 1, EG - 1:EG], -1).then_inc(s_set, 1)
            dve.wait_ge(s_in, 16 * (2 + 4 * GC))
            cnt.mark(dve.tensor_copy(val[:, 1, :, :], raw[:, 1, :, :]))
            cnt.mark(dve.tensor_tensor(val[:, 2, :, :], raw[:, 0, :, :], raw[:, 2, :, :], ALU.not_equal))
            cnt.mark(dve.tensor_tensor(val[:, 3, :, :], raw[:, 0, :, :], raw[:, 3, :, :], ALU.not_equal))
            cnt.chain(dve.tensor_copy(val[:, 0, :, :], raw[:, 0, :, :]))
            dve.wait_ge(s_io, 3)
            for cc in range(GC):
                at = cnt.mark(dve.tensor_scalar(le[:, cc, :], thr[:, :], val[:, 0, cc, EG - 1:EG], None, ALU.is_le))
            dve.wait_ge(s_v, at)
            cnt.chain(dve.tensor_reduce(last[:, :], le[:, :, :], AX, ALU.add))
            cnt.chain(dve.tensor_tensor(last[:, :], last[:, :], gid[:, :], ALU.add))
            for cc in range(GC):
                m = dve.tensor_scalar(past[:, cc, :], steps[0:GP, :], last[:, cc:cc + 1], None, ALU.is_gt)
            m.then_inc(s_past, 1)
            dve.wait_ge(s_cnt, 1)
            cnt.chain(dve.tensor_scalar(gq[:, :], ps[7][:, 0:NSTEP], float(NG - 1), None, ALU.min))
            cnt.chain(dve.tensor_tensor(nq[:, :], steps[:, :], gq[:, :], ALU.subtract))
            for cc in range(GC):
                m = dve.tensor_scalar(pick[:, cc, :], gq[0:GP, :], gid[:, cc:cc + 1], None, ALU.is_equal)
            m.then_inc(s_pick, 1)

            def pair(x):
                return x.rearrange("p (q j) -> p q j", j=2)

            dve.wait_ge(s_got, 1)
            for j in range(2):
                dve.tensor_copy(pair(st.src[:, :])[:, :, j], ps[2 + j][0:P, 0:NSTEP])
                cnt.mark(dve.scalar_tensor_tensor(pair(st.row[:, :])[:, :, j], nq[0:P, :], -float(P),
                                                  ps[j][0:P, 0:NSTEP], ALU.mult, ALU.add))
                for f in range(2):
                    dve.tensor_scalar(pair(st.breaks[:, f, :])[:, :, j], ps[4 + 2 * f + j][0:P, 0:NSTEP],
                                      NEG, None, ALU.mult)
            dve.wait_ge(s_v, cnt.at)
            cnt.mark(dve.tensor_scalar(m2[:, 0, :], st.row[:, :], 0.0, NEG, ALU.is_lt, ALU.mult))
            cnt.chain(dve.tensor_scalar(m2[:, 1, :], st.row[:, :], float(P - 1), NEG, ALU.is_gt, ALU.mult))
            dve.tensor_tensor(st.mask[:, :], m2[:, 0, :], m2[:, 1, :], ALU.add)
            cnt.chain(dve.tensor_scalar(nq[:, :], nq[:, :], float(NT - 1), None, ALU.min))
            dve.tensor_copy(st.tile[:, :], nq[0:1, :])
            dve.memset(st.keep[:, 0:1], 0.0)
            dve.tensor_tensor(st.keep[:, 1:NSTEP], nq[0:P, 1:NSTEP], nq[0:P, 0:NSTEP - 1], ALU.is_equal)

        @block.tensor
        def _(pe):
            pe.wait_ge(s_past, 1)
            for cc in range(GC):
                m = pe.matmul(ps[7][:, 0:NSTEP], c.ones[0:GP, :], past[:, cc, :], start=cc == 0, stop=cc == GC - 1)
            m.then_inc(s_cnt, 1)
            pe.wait_ge(s_pick, 1)
            for a in range(4):
                for j in range(2):
                    for cc in range(GC):
                        m = pe.matmul(ps[2 * a + j][0:P, 0:NSTEP], val[:, a, cc, j * P:(j + 1) * P], pick[:, cc, :],
                                      start=cc == 0, stop=cc == GC - 1)
            m.then_inc(s_got, 1)


def edge_phase(nc, c, st, kv_d):
    with ExitStack() as ctx:
        def sb(name, shape, dt=F32):
            return ctx.enter_context(nc.sbuf_tensor("e_" + name, shape, dt))

        def ps(name):
            return ctx.enter_context(nc.psum_tensor("e_" + name, [128, 512], F32))

        def sem(name):
            return ctx.enter_context(nc.semaphore("e_" + name))

        kv = sb("kv", [P, RING, SPC, 2, 2 * D])
        idx = sb("idx", [P, RING, T], I32)
        oh = sb("oh", [P, RING, SPC, 2, P])
        ohT = sb("ohT", [P, 2, 2, P])
        prod = sb("prod", [P, 2, D])
        score = sb("score", [P, RING, H, T])
        masked = sb("masked", [P, H, T])
        marks = sb("marks", [P, 2, H, T])
        marksT = sb("marksT", [R, 2, P])
        mark_sum = sb("mark_sum", [R, 2])
        fwd = sb("fwd", [R, P])
        bwd = sb("bwd", [R, P])
        carry_in = sb("carry_in", [R, 2])
        seg = sb("seg", [R, P])
        ex = sb("ex", [P, RING, H, T])
        row = sb("rows", [1, 6, H, T + 1])
        before = sb("before", [1, 2, H, T])
        fix = sb("fix", [1, 3, H])
        scale = sb("scale", [P, H])
        wv = sb("wv", [P, 2, 2, SLOT])
        pq = [ps(f"pq{b}") for b in range(2)]
        pa = [ps(f"pa{b}") for b in range(2)]
        pt = [ps(f"pt{b}") for b in range(2)]
        pS, pX = ps("pS"), ps("pX")
        ptv = [pt[b][0:P, 0:2 * P].rearrange("p (j n) -> p j n", j=2) for b in range(2)]
        scoreT = pS[0:R, 0:P]
        marksP = pS[0:R, P:3 * P].rearrange("p (f e) -> p f e", f=2)
        pR = pS[0:1, P:P + 5 * R]
        rows3 = pR[:, 0:3 * R].rearrange("p (a h t) -> p a h t", a=3, h=H)
        rowb = pR[:, 3 * R:4 * R].rearrange("p (h t) -> p h t", h=H)
        rowm = pR[:, 4 * R:5 * R].rearrange("p (h t) -> p h t", h=H)
        exT = pX[0:P, 0:R]
        cinT = [pS[0:R, 500 + k:501 + k] for k in range(2)]
        growT = pX[0:P, 136:136 + H]
        RF0, RF1, RFO, RB0, RB1, RBO = range(6)

        s_gath = [[sem(f"rows_in{r}_{s}") for s in range(SPC)] for r in range(RING)]
        names = ("idx_staged", "gather_go", "onehot", "onehotT_psum", "onehotT", "query_rows", "prod", "scored",
                 "masked", "marks", "scoreT", "marksT", "fwd_own", "ends", "fwd_rows", "fwd_carry", "bwd_own",
                 "starts", "bwd_rows", "bwd_carry", "segmax", "shifted", "exped", "maxrow", "exT", "ex",
                 "fixarg", "fixexp", "fixrow", "fixcol", "scale", "rescaled", "weighted", "summed", "added", "link", "turn_go")
        S = {n: sem(n) for n in names}
        block = ctx.enter_context(nc.Block())

        @block.gpsimd
        def _(pool):
            def gather(k):
                for s in range(SPC):
                    free = (k.c - RING) * SPC + s + 1
                    if s == 0:
                        wait(pool, S["weighted"], free)
                        pool.tensor_copy(idx[:, k.ring, :], st.src[:, ds(k.c * T, T)]).then_inc(S["idx_staged"], 1)
                        pool.wait_ge(S["idx_staged"], k.c + 1)
                    else:
                        wait(pool, S["weighted"], free)
                    pool.sem_inc(S["gather_go"], 1)
                    for j in range(2):
                        pool.indirect_dma_start(
                            out=kv[:, k.ring, s, j, :], out_offset=None, in_=kv_d[:, :],
                            in_offset=bass.IndirectOffsetOnAxis(ap=idx[:, k.ring, 2 * s + j:2 * s + j + 1], axis=0)
                        ).then_inc(s_gath[k.ring][s], 16)

            for k in range(RING):
                gather(Chunk(0, k))
            with pool.Fori(1, NCH // RING) as i:
                for u in range(RING):
                    gather(Chunk(i, u))

        @block.vector
        def _(dve):
            cnt = Count(dve, S["link"])
            for a in (RF0, RF1, RB0, RB1):
                cnt.mark(dve.memset(row[:, a, :, :], NEG))
            dve.wait_ge(S["link"], cnt.at)

            def onehot(k, s):
                wait(dve, S["summed"], (k.c - RING) * SPC + s + 1)
                for j in range(2):
                    m = dve.tensor_scalar(oh[:, k.ring, s, j, :], c.iota[0:P, 0:P],
                                          st.row[:, ds((k.c * SPC + s) * 2 + j, 1)], None, ALU.is_equal)
                m.then_inc(S["onehot"], 1)

            def score_step(k, s):
                q = k.c * SPC + s
                dve.wait_ge(S["query_rows"], q + 1)
                dve.wait_ge(s_gath[k.ring][s], 32 * k.turn + 32)
                wait(dve, S["scored"], q)
                dve.tensor_tensor(prod[:, :, :], pq[s % 2][0:P, :].rearrange("p (j d) -> p j d", j=2),
                                  kv[:, k.ring, s, :, 0:D], ALU.mult).then_inc(S["prod"], 1)
                dve.wait_ge(S["prod"], q + 1)
                dve.tensor_reduce(score[:, k.ring, :, 2 * s:2 * s + 2].rearrange("p h j -> p j h"),
                                  prod[:, :, :].rearrange("p j (h d) -> p j h d", h=H), AX, ALU.add
                                  ).then_inc(S["scored"], 1)

            def add_step(k, s, n):
                q = k.c * SPC + s
                wait(dve, S["added"], q)
                slot = c.slots[:, ds(n, 1), :].rearrange("p a v -> p (a v)")
                if s == 0 and k.within(1, NCH):
                    dve.wait_ge(S["scale"], k.c)
                    dve.tensor_tensor(slot.rearrange("p (h v) -> p h v", h=H), slot.rearrange("p (h v) -> p h v", h=H),
                                      scale[:, :].unsqueeze(2).broadcast_to([P, H, VH]),
                                      ALU.mult).then_inc(S["rescaled"], 1)
                    dve.wait_ge(S["rescaled"], k.c)
                dve.wait_ge(S["summed"], q + 1)
                dve.scalar_tensor_tensor(slot, slot, st.keep[:, ds(q, 1)], pa[s % 2][0:P, 0:SLOT],
                                         ALU.mult, ALU.add).then_inc(S["added"], 1)

            def softmax_stage(k, s):
                if s == 0:
                    dve.wait_ge(S["scored"], (k.c + 1) * SPC)
                    wait(dve, S["scoreT"], k.c)
                    dve.tensor_tensor(masked[:, :, :], score[:, k.ring, :, :],
                                      st.mask[:, ds(k.c * T, T)].unsqueeze(1).broadcast_to([P, H, T]),
                                      ALU.add).then_inc(S["masked"], 1)
                if s == 2:
                    dve.wait_ge(S["marksT"], k.c + 1)
                    dve.tensor_tensor_scan(fwd[:, :], marksT[:, 0, :], scoreT, NEG, ALU.add, ALU.max
                                           ).then_inc(S["fwd_own"], 1)
                if s == 3:
                    dve.wait_ge(S["ends"], k.c + 1)
                    if k.within(1, NCH):
                        dve.wait_ge(S["fwd_rows"], 3 * k.c)
                        dve.tensor_copy(row[:, RF1, :, 0], row[:, RFO, :, T])
                    dve.tensor_copy(row[:, RF1, :, 1:T + 1], rows3[:, 0, :, :])
                    dve.tensor_copy(row[:, RB0, :, 0:T], rows3[:, 2, :, :])
                    dve.tensor_copy(row[:, RF0, :, 1:T + 1], rows3[:, 1, :, :]).then_inc(S["fwd_rows"], 1)
                    dve.wait_ge(S["fwd_rows"], 3 * k.c + 1)
                    dve.tensor_tensor_scan(flat(RFO), flat(RF0), flat(RF1), NEG, ALU.add, ALU.max
                                           ).then_inc(S["fwd_rows"], 1)
                    dve.wait_ge(S["fwd_rows"], 3 * k.c + 2)
                    dve.tensor_copy(before[:, 0, :, :], row[:, RFO, :, 0:T]).then_inc(S["fwd_rows"], 1)
                if s == 4:
                    dve.wait_ge(S["fwd_carry"], k.c + 1)
                    dve.tensor_copy(carry_in[:, 0:1], cinT[0]).then_inc(S["segmax"], 1)
                    dve.wait_ge(S["segmax"], 4 * k.c + 1)
                    dve.tensor_tensor_scan(fwd[:, :], marksT[:, 0, :], scoreT, carry_in[:, 0:1], ALU.add, ALU.max
                                           ).then_inc(S["segmax"], 1)
                    dve.wait_ge(S["segmax"], 4 * k.c + 2)
                    dve.tensor_tensor_scan(bwd[:, ::-1], marksT[:, 1, ::-1], fwd[:, ::-1], NEG, ALU.add, ALU.max
                                           ).then_inc(S["bwd_own"], 1)
                if s == 5:
                    dve.wait_ge(S["starts"], k.c + 1)
                    dve.tensor_copy(row[:, RB1, :, 0:T], rowb).then_inc(S["bwd_rows"], 1)
                    dve.wait_ge(S["bwd_rows"], 3 * k.c + 1)
                    dve.tensor_tensor_scan(flat(RBO)[:, ::-1], flat(RB0)[:, ::-1], flat(RB1)[:, ::-1], NEG,
                                           ALU.add, ALU.max).then_inc(S["bwd_rows"], 1)
                    dve.wait_ge(S["bwd_rows"], 3 * k.c + 2)
                    dve.tensor_copy(before[:, 1, :, :], row[:, RBO, :, 1:T + 1]).then_inc(S["bwd_rows"], 1)
                if s == 6:
                    dve.wait_ge(S["bwd_carry"], k.c + 1)
                    dve.tensor_copy(carry_in[:, 1:2], cinT[1]).then_inc(S["segmax"], 1)
                    dve.wait_ge(S["segmax"], 4 * k.c + 3)
                    dve.tensor_tensor_scan(bwd[:, ::-1], marksT[:, 1, ::-1], fwd[:, ::-1], carry_in[:, 1:2],
                                           ALU.add, ALU.max).then_inc(S["segmax"], 1)
                    dve.wait_ge(S["segmax"], 4 * k.c + 4)
                    wait(dve, S["exT"], k.c)
                    dve.tensor_tensor(seg[:, :], scoreT, bwd[:, :], ALU.subtract).then_inc(S["shifted"], 1)
                if s == 7:
                    dve.wait_ge(S["maxrow"], k.c + 1)
                    wait(dve, S["fixexp"], k.c)
                    dve.tensor_tensor(fix[:, 0, :], row[:, RF1, :, 0], rowm[:, :, 0],
                                      ALU.subtract).then_inc(S["link"], 1)
                    dve.wait_ge(S["link"], k.c + 5)
                    dve.scalar_tensor_tensor(fix[:, 1, :], marks[0:1, 0, :, 0], 0.0, fix[:, 0, :],
                                             ALU.is_equal, ALU.mult).then_inc(S["fixarg"], 1)

            def flat(a):
                return row[:, a, :, :].rearrange("p h t -> p (h t)")

            def rescale_row(k):
                dve.wait_ge(S["fixexp"], k.c + 1)
                dve.tensor_scalar(fix[:, 2, :], fix[:, 2, :], -1.0, None, ALU.add).then_inc(S["fixrow"], 1)

            def rescale_col(k):
                dve.wait_ge(S["fixcol"], k.c)
                dve.tensor_scalar(scale[:, :], growT, 1.0, None, ALU.add).then_inc(S["scale"], 1)

            def body(k):
                nxt, prv = k.plus(1), k.plus(-1)
                for s in range(SPC):
                    add = prv.step(s - 3)
                    if add:
                        n = dve.value_load(st.tile[0:1, ds(add[0].c * SPC + add[1], 1)], min_val=0, max_val=NT - 1)
                    if s == 1 and prv.within(1, NCH):
                        rescale_row(prv)
                    if nxt.step(s - 1):
                        score_step(*nxt.step(s - 1))
                    if nxt.step(s + 3):
                        onehot(*nxt.step(s + 3))
                    if add:
                        add_step(*add, n)
                    if s == 2 and prv.within(1, NCH):
                        rescale_col(prv)
                    if k.within(0, NCH):
                        softmax_stage(k, s)

            for s in range(3):
                onehot(Chunk(0, 0), s)
            chunk_bodies(dve, body)

        @block.scalar
        def _(act):
            def weight(k, s):
                q = k.c * SPC + s
                act.wait_ge(S["ex"], k.c + 1)
                wait(act, S["summed"], q - 1)
                w4 = wv[:, s % 2, :, :].rearrange("p j (h v) -> p j h v", h=H)
                for j in range(2):
                    for h in range(H):
                        act.activation(w4[:, j, h, 0:HD], kv[:, k.ring, s, j, D + h * HD:D + (h + 1) * HD],
                                       ACT.Copy, scale=ex[:, k.ring, h, 2 * s + j:2 * s + j + 1])
                act.activation(w4[:, :, :, HD], ex[:, k.ring, :, 2 * s:2 * s + 2].rearrange("p h j -> p j h"),
                               ACT.Copy).then_inc(S["weighted"], 1)

            def keep_onehotT(k, s):
                q = k.c * SPC + s
                act.wait_ge(S["onehotT_psum"], q + 1)
                wait(act, S["query_rows"], q - 1)
                act.activation(ohT[:, s % 2, :, :], ptv[s % 2], ACT.Copy).then_inc(S["onehotT"], 1)

            def softmax_stage(k, s):
                if s == 0:
                    wait(act, S["fixarg"], k.c)
                    wait(act, S["scoreT"], k.c)
                    act.activation(marks[:, :, :, :],
                                   st.breaks[:, :, ds(k.c * T, T)].unsqueeze(2).broadcast_to([P, 2, H, T]),
                                   ACT.Copy).then_inc(S["marks"], 1)
                if s == 1:
                    act.wait_ge(S["scoreT"], k.c + 1)
                    wait(act, S["shifted"], k.c)
                    for f in range(2):
                        m = act.activation(marksT[:, f, :], marksP[:, f, :], ACT.Copy,
                                           accum_out=mark_sum[:, f:f + 1])
                    m.then_inc(S["marksT"], 1)

            def softmax_exp(k):
                act.wait_ge(S["shifted"], k.c + 1)
                act.activation(seg[:, :], seg[:, :], ACT.Exp, scale=HD ** -0.5).then_inc(S["exped"], 1)

            def softmax_kept(k):
                act.wait_ge(S["exT"], k.c + 1)
                act.activation(ex[:, k.ring, :, :].rearrange("p h t -> p (h t)"), exT, ACT.Copy
                               ).then_inc(S["ex"], 1)
                act.wait_ge(S["fixarg"], k.c + 1)
                wait(act, S["fixcol"], k.c - 1)
                act.activation(fix[:, 2, :], fix[:, 1, :], ACT.Exp, scale=HD ** -0.5).then_inc(S["fixexp"], 1)

            def body(k):
                nxt, prv = k.plus(1), k.plus(-1)
                for s in range(SPC):
                    if s == SPC - 1 and k.within(0, NCH):
                        softmax_exp(k)
                    if nxt.step(s + 1):
                        keep_onehotT(*nxt.step(s + 1))
                    if prv.step(s - 1):
                        weight(*prv.step(s - 1))
                    if s == 0 and prv.within(0, NCH):
                        softmax_kept(prv)
                    if k.within(0, NCH):
                        softmax_stage(k, s)

            keep_onehotT(Chunk(0, 0), 0)
            chunk_bodies(act, body)

        @block.tensor
        def _(pe):
            def turn_onehot(k, s):
                q = k.c * SPC + s
                pe.wait_ge(S["onehot"], q + 1)
                wait(pe, S["onehotT"], q - 1)
                for j in range(2):
                    m = pe.transpose(ptv[s % 2][:, j, :], oh[:, k.ring, s, j, :], c.ident[0:P, 0:P])
                m.then_inc(S["onehotT_psum"], 1)

            def query_rows(k, s, n):
                q = k.c * SPC + s
                pe.wait_ge(S["onehotT"], q + 1)
                wait(pe, S["prod"], q - 1)
                for j in range(2):
                    m = pe.matmul(pq[s % 2][0:P, j * D:(j + 1) * D], ohT[:, s % 2, j, :],
                                  c.slots[:, ds(n + 1, 1), 0:D].rearrange("p a d -> p (a d)"), start=True, stop=True)
                m.then_inc(S["query_rows"], 1)

            def sum_step(k, s):
                q = k.c * SPC + s
                pe.wait_ge(S["weighted"], q + 1)
                wait(pe, S["added"], q - 1)
                for j in range(2):
                    m = pe.matmul(pa[s % 2][0:P, 0:SLOT], oh[:, k.ring, s, j, :], wv[:, s % 2, j, :],
                                  start=j == 0, stop=j == 1)
                m.then_inc(S["summed"], 1)

            idR = c.ident[0:R, 0:R]

            def softmax_stage(k, s):
                if s == 1:
                    pe.wait_ge(S["masked"], k.c + 1)
                    pe.wait_ge(S["marks"], k.c + 1)
                    wait(pe, S["shifted"], k.c)
                    wait(pe, S["marksT"], k.c)
                    pe.sem_inc(S["turn_go"], 1)
                    pe.transpose(scoreT, masked[:, :, :].rearrange("p h t -> p (h t)"), c.ident[0:P, 0:P])
                    for f in range(2):
                        m = pe.transpose(marksP[:, f, :], marks[:, f, :, :].rearrange("p h t -> p (h t)"),
                                         c.ident[0:P, 0:P])
                    m.then_inc(S["scoreT"], 1)
                if s == 3:
                    pe.wait_ge(S["fwd_own"], k.c + 1)
                    pe.wait_ge(S["marksT"], k.c + 1)
                    pe.sem_inc(S["turn_go"], 1)
                    for a, col in enumerate((fwd[:, P - 1:P], mark_sum[:, 0:1], mark_sum[:, 1:2])):
                        m = pe.transpose(pR[:, a * R:(a + 1) * R], col, idR)
                    m.then_inc(S["ends"], 1)
                if s == 4:
                    pe.wait_ge(S["fwd_rows"], 3 * k.c + 3)
                    pe.sem_inc(S["turn_go"], 1)
                    pe.transpose(cinT[0], before[:, 0, :, :].rearrange("p h t -> p (h t)"), c.ident[0:1, 0:1]).then_inc(S["fwd_carry"], 1)
                if s == 5:
                    pe.wait_ge(S["bwd_own"], k.c + 1)
                    pe.sem_inc(S["turn_go"], 1)
                    pe.transpose(pR[:, 3 * R:4 * R], bwd[:, 0:1], idR).then_inc(S["starts"], 1)
                if s == 6:
                    pe.wait_ge(S["bwd_rows"], 3 * k.c + 3)
                    pe.sem_inc(S["turn_go"], 1)
                    pe.transpose(cinT[1], before[:, 1, :, :].rearrange("p h t -> p (h t)"), c.ident[0:1, 0:1]).then_inc(S["bwd_carry"], 1)
                if s == 7:
                    pe.wait_ge(S["shifted"], k.c + 1)
                    wait(pe, S["fixarg"], k.c)
                    pe.sem_inc(S["turn_go"], 1)
                    pe.transpose(pR[:, 4 * R:5 * R], bwd[:, 0:1], idR).then_inc(S["maxrow"], 1)

            def exp_back(k):
                pe.wait_ge(S["exped"], k.c + 1)
                wait(pe, S["ex"], k.c)
                pe.sem_inc(S["turn_go"], 1)
                pe.transpose(exT, seg[:, :], idR).then_inc(S["exT"], 1)

            def body(k):
                nxt, prv = k.plus(1), k.plus(-1)
                for s in range(SPC):
                    if nxt.within(0, NCH):
                        n = pe.value_load(st.tile[0:1, ds(nxt.c * SPC + s, 1)], min_val=0, max_val=NT - 1)
                    if s == 0 and prv.within(0, NCH):
                        exp_back(prv)
                    if s == 2 and prv.within(1, NCH):
                        pe.wait_ge(S["fixrow"], prv.c)
                        wait(pe, S["scale"], prv.c - 1)
                        pe.matmul(growT, oh[0:1, prv.ring, 0, 0, :], fix[:, 2, :], start=True, stop=True
                                  ).then_inc(S["fixcol"], 1)
                    if k.within(0, NCH):
                        softmax_stage(k, s)
                    if nxt.step(s + 2):
                        turn_onehot(*nxt.step(s + 2))
                    if nxt.within(0, NCH):
                        query_rows(nxt, s, n)
                    if prv.step(s - 2):
                        sum_step(*prv.step(s - 2))

            for s in range(2):
                turn_onehot(Chunk(0, 0), s)
            chunk_bodies(pe, body)


def dense_phase(nc, c, w, s1_d, qm_d, out):
    with ExitStack() as ctx:
        def sb(name, shape, dt=F32):
            return ctx.enter_context(nc.sbuf_tensor("d_" + name, shape, dt))

        def ps(name):
            return ctx.enter_context(nc.psum_tensor("d_" + name, [128, 512], F32))

        def sem(name):
            return ctx.enter_context(nc.semaphore("d_" + name))

        W1, W2 = sb("W1", [128, KC, FF]), sb("W2", [128, NF, D])
        We1, We2 = sb("We1", [128, NE, KC, D]), sb("We2", [128, NE, KC, D])
        bf1, be1 = sb("bf1", [128, NF]), sb("be1", [128, NE, KC])
        be2 = sb("be2", [NE, D])
        wr, wrT = sb("wr", [NE, D]), sb("wrT", [128, KC, NE])
        rows = sb("rows", [P, 6, D])
        LG1, LB1, FB2, LG2, LB2, GAM = range(6)
        s1, qm, xt = (sb(n, [P, 2, 2, D]) for n in ("s1", "qm", "xt"))
        r, h, hb, mix, tok = (sb(n, [P, 2, D]) for n in ("r", "h", "hb", "mix", "tok"))
        acc = sb("acc", [P, 2, 2, D])
        qT, hT = (sb(n, [128, KC, 2 * P]) for n in ("qT", "hT"))
        tokT = sb("tokT", [128, 2, KC, 2 * P])
        fT = sb("fT", [128, NF, 2 * P])
        eT = sb("eT", [128, 2, KC, 2 * P])
        den = sb("den", [P, 2, 2, H])
        st, mv, nw = sb("st", [P, 2, 6]), sb("mv", [P, 2, 2]), sb("nw", [P, 3, 2])
        pr = sb("pr", [P, 2, NE])
        pm = sb("pm", [P, 4, 2])
        top = sb("top", [P, 2, 8])
        topi = sb("topi", [P, 2, 8], U32)
        topf = sb("topf", [P, 2, 2])
        tw = sb("tw", [P, 2, 2])
        hit = sb("hit", [P, 2, 2, NE])
        comb = sb("comb", [P, 2, 2, NE])
        combT = sb("combT", [NE, 2 * P])
        cell = sb("cell", [1, 1])
        ph = [ps(f"ph{b}") for b in range(2)]
        py = [ps(f"py{b}") for b in range(2)]
        pT = [ps(f"pT{b}") for b in range(2)]
        pw, pl = ps("pw"), ps("pl")

        s_w, s_c = sem("weights_in"), sem("small_in")
        s_s1, s_qm, s_x = ([sem(f"{n}_in{b}") for b in range(2)] for n in ("s1", "qm", "x"))
        s_out = [sem(f"out{b}") for b in range(2)]
        names = ("link", "h", "hb", "mixn", "mixx", "r2", "tok", "accinit", "acc", "comb", "logit_shift", "logit_exp",
                 "qT_psum", "qT", "hT_psum", "hT", "tokT_psum", "tokT", "mixed", "ffn", "hidden", "gelu", "y",
                 "logits", "combT_psum", "combT", "wrT_psum", "wrT")
        S = {n: sem(n) for n in names}
        block = ctx.enter_context(nc.Block())

        def pair(x):
            return x[0:P, :].rearrange("p (t d) -> p t d", t=2)

        def bcast(k):
            return rows[:, k, :].unsqueeze(1).broadcast_to([P, 2, D])

        def hidden_base(g):
            return 0 if isinstance(g.i, int) and g.i == 0 else HB_BODY * g.i - (HB_BODY - NF)

        @block.sync
        def _(sp):
            def load(g):
                for dst, src, s, used, count in ((s1, s1_d, s_s1, "h", g.i - 1), (qm, qm_d, s_qm, "qT_psum", g.i - 1),
                                                 (xt, w["x"], s_x, "mixx", 2 * (g.i - 1))):
                    wait(sp, S[used], count)
                    sp.dma_start(dst[:, g.b, :, :],
                                 src[ds(g.i * (2 * P), 2 * P), :].rearrange("(t p) d -> p t d", p=P)).then_inc(s[g.b], 16)

            def store(g):
                sp.wait_ge(S["acc"], (g.i + 1) * ACC_STEPS)
                sp.dma_start(out[ds(g.i * (2 * P), 2 * P), :].rearrange("(t p) d -> p t d", p=P),
                             acc[:, g.b, :, :]).then_inc(s_out[g.b], 16)

            load(Group(0, 0))
            for k, name in enumerate(("ln1_g", "ln1_b", "b2", "ln2_g", "ln2_b")):
                sp.dma_start(rows[:, k, :], w["L0_gnn_" + name].partition_broadcast(P)).then_inc(s_c, 16)
            sp.dma_start(rows[:, GAM, :], w["L0_mix_gamma"].partition_broadcast(P)).then_inc(s_c, 16)
            sp.dma_start(wr[:, :], w["L0_ffn_router_w"]).then_inc(s_c, 16)
            sp.dma_start(be2[:, :], w["L0_ffn_b2"]).then_inc(s_c, 16)
            with nc.allow_non_contiguous_dma("biases by column, a few KB"):
                sp.dma_start(bf1[:, :], w["L0_gnn_b1"].rearrange("(f p) -> p f", p=128)).then_inc(s_c, 16)
                for e in range(NE):
                    sp.dma_start(be1[:, e, :], w["L0_ffn_b1"][e, :].rearrange("(c p) -> p c", p=128)).then_inc(s_c, 16)
            sp.dma_start(W1[:, :, :], w["L0_gnn_W1"].rearrange("(c p) n -> p c n", p=128)).then_inc(s_w, 16)
            sp.dma_start(W2[:, :, :], w["L0_gnn_W2"].rearrange("(c p) n -> p c n", p=128)).then_inc(s_w, 16)
            for e in range(NE):
                sp.dma_start(We1[:, e, :, :], w["L0_ffn_w1"][e, :, :].rearrange("(c p) n -> p c n", p=128)).then_inc(s_w, 16)
                sp.dma_start(We2[:, e, :, :], w["L0_ffn_w2"][e, :, :].rearrange("(c p) n -> p c n", p=128)).then_inc(s_w, 16)
            load(Group(0, 1))

            def body(g):
                if g.within(1, NGR - 1):
                    load(g.plus(1))
                if g.within(1, NGR + 1):
                    store(g.plus(-1))

            group_bodies(sp, body, 1)
            for b in range(2):
                sp.wait_ge(s_out[b], 16 * ((NGR + 1 - b) // 2))

        @block.gpsimd
        def _(pool):
            pool.wait_ge(s_c, 16 * NSMALL)

            def body(g):
                if not g.within(0, NGR):
                    return
                pool.wait_ge(S["h"], g.i + 1)
                wait(pool, S["r2"], g.i)
                pool.tensor_tensor(hb[:, :, :], h[:, :, :], bcast(FB2), ALU.add).then_inc(S["hb"], 1)
                pool.wait_ge(S["mixn"], g.i + 1)
                pool.tensor_tensor(mix[:, :, :], mix[:, :, :], bcast(GAM), ALU.mult).then_inc(S["mixx"], 1)
                pool.wait_ge(S["mixx"], 2 * g.i + 1)
                pool.wait_ge(s_x[g.b], 16 * g.turn + 16)
                pool.tensor_tensor(mix[:, :, :], mix[:, :, :], xt[:, g.b, :, :], ALU.add).then_inc(S["mixx"], 1)

            group_bodies(pool, body, 1)

        @block.vector
        def _(dve):
            def norm(cnt, src, dst, last, sem_last):
                for t in range(2):
                    at = cnt.mark(dve.bn_stats(st[:, t, :], src[:, t, :]))
                dve.wait_ge(S["link"], at)
                for t in range(2):
                    if t == 0:
                        hold(dve, cell[:, :])
                    cnt.mark(dve.bn_aggr(mv[:, t, :], st[:, t, :]))
                dve.wait_ge(S["link"], cnt.at)
                rsqrt_newton(dve, cnt, mv[:, :, 1], nw[:, 0, :], nw[:, 1, :], nw[:, 2, :])
                if last:
                    last()
                for t in range(2):
                    m = dve.tensor_scalar(dst[:, t, :], src[:, t, :], mv[:, t, 0:1], nw[:, 1, t:t + 1],
                                          ALU.subtract, ALU.mult)
                m.then_inc(sem_last, 1)

            def hidden_state(g, cnt):
                slot = c.slots[:, ds(2 * g.i, 2), :].rearrange("p t (h v) -> p t h v", h=H)
                cnt.chain(dve.tensor_scalar(den[:, 0, :, :], slot[:, :, :, HD], 1e-16, None, ALU.add))
                cnt.chain(dve.reciprocal(den[:, 1, :, :], den[:, 0, :, :]))
                r4 = r[:, :, :].rearrange("p t (h v) -> p t h v", h=H)
                for t in range(2):
                    cnt.mark(dve.tensor_tensor(r4[:, t], slot[:, t, :, 0:HD],
                                               den[:, 1, t, :].unsqueeze(2).broadcast_to([P, H, HD]), ALU.mult))
                dve.wait_ge(S["link"], cnt.at)
                dve.wait_ge(s_s1[g.b], 16 * g.turn + 16)
                cnt.chain(dve.tensor_tensor(r[:, :, :], r[:, :, :], s1[:, g.b, :, :], ALU.add))
                if not (isinstance(g.i, int) and g.i == 0):
                    free = lambda: (dve.wait_ge(S["hT_psum"], g.i), dve.wait_ge(S["hb"], g.i))
                else:
                    free = None
                norm(cnt, r, h, free, S["link"])
                cnt.at = cnt.at + 1
                dve.wait_ge(S["link"], cnt.at)
                cnt.chain(dve.tensor_tensor(h[:, :, :], h[:, :, :], bcast(LG1), ALU.mult))
                dve.tensor_tensor(h[:, :, :], h[:, :, :], bcast(LB1), ALU.add).then_inc(S["h"], 1)

            def mix_norm(g, cnt):
                dve.wait_ge(S["mixed"], g.i + 1)
                norm(cnt, pair(pw), mix, None, S["mixn"])

            def tokens(g, cnt):
                dve.wait_ge(S["ffn"], g.i + 1)
                dve.wait_ge(S["hb"], g.i + 1)
                dve.tensor_tensor(r[:, :, :], pair(pw), hb[:, :, :], ALU.add).then_inc(S["r2"], 1)
                dve.wait_ge(S["r2"], g.i + 1)
                norm(cnt, r, r, None, S["link"])
                cnt.at = cnt.at + 1
                dve.wait_ge(S["link"], cnt.at)
                cnt.chain(dve.tensor_tensor(r[:, :, :], r[:, :, :], bcast(LG2), ALU.mult))
                cnt.chain(dve.tensor_tensor(r[:, :, :], r[:, :, :], bcast(LB2), ALU.add))
                dve.wait_ge(S["mixx"], 2 * g.i + 2)
                cnt.chain(dve.tensor_tensor(r[:, :, :], r[:, :, :], mix[:, :, :], ALU.add))
                norm(cnt, r, tok, None, S["tok"])
                dve.wait_ge(S["tok"], g.i + 1)
                if g.within(2, NGR):
                    dve.wait_ge(s_out[g.b], 16 * g.turn)
                dve.tensor_tensor(acc[:, g.b, :, :], r[:, :, :], tok[:, :, :], ALU.add).then_inc(S["accinit"], 1)

            def route(g, cnt):
                lg = pl[0:P, 0:2 * NE].rearrange("p (t e) -> p t e", t=2)
                dve.wait_ge(S["logits"], g.i + 1)
                cnt.chain(dve.tensor_reduce(pm[:, 0, :], lg, AX, ALU.max))
                dve.tensor_tensor(pr[:, :, :], lg, pm[:, 0, :].unsqueeze(2).broadcast_to([P, 2, NE]),
                                  ALU.subtract).then_inc(S["logit_shift"], 1)
                dve.wait_ge(S["logit_exp"], g.i + 1)
                cnt.chain(dve.tensor_reduce(pm[:, 1, :], pr[:, :, :], AX, ALU.add))
                cnt.chain(dve.reciprocal(pm[:, 2, :], pm[:, 1, :]))
                cnt.chain(dve.tensor_tensor(pr[:, :, :], pr[:, :, :],
                                            pm[:, 2, :].unsqueeze(2).broadcast_to([P, 2, NE]), ALU.mult))
                hold(dve, cell[:, :])
                for t in range(2):
                    cnt.mark(dve.max(top[:, t, :], pr[:, t, :]))
                dve.wait_ge(S["link"], cnt.at)
                hold(dve, cell[:, :])
                for t in range(2):
                    cnt.mark(dve.max_index(topi[:, t, :], top[:, t, :], pr[:, t, :]))
                dve.wait_ge(S["link"], cnt.at)
                cnt.mark(dve.tensor_copy(topf[:, :, :], topi[:, :, 0:2]))
                cnt.chain(dve.tensor_tensor(pm[:, 3, :], top[:, :, 0], top[:, :, 1], ALU.add))
                cnt.chain(dve.tensor_scalar(pm[:, 3, :], pm[:, 3, :], 1e-12, None, ALU.max))
                cnt.chain(dve.reciprocal(pm[:, 2, :], pm[:, 3, :]))
                cnt.chain(dve.tensor_tensor(tw[:, :, :], top[:, :, 0:2],
                                            pm[:, 2, :].unsqueeze(2).broadcast_to([P, 2, 2]), ALU.mult))
                for t in range(2):
                    for k in range(2):
                        cnt.mark(dve.tensor_scalar(hit[:, k, t, :], c.iota[0:P, 0:NE], topf[:, t, k:k + 1],
                                                   tw[:, t, k:k + 1], ALU.is_equal, ALU.mult))
                dve.wait_ge(S["link"], cnt.at)
                dve.tensor_tensor(comb[:, g.b, :, :], hit[:, 0, :, :], hit[:, 1, :, :], ALU.add).then_inc(S["comb"], 1)

            def accumulate(m, e):
                y = m.i * (NE + 1) + e
                dve.wait_ge(S["y"], y + 1)
                p = pair(py[(m.b + e) % 2])
                if e == NE:
                    dve.wait_ge(S["acc"], m.i * ACC_STEPS + e)
                    dve.tensor_tensor(acc[:, m.b, :, :], acc[:, m.b, :, :], p, ALU.add).then_inc(S["acc"], 1)
                    return
                if e:
                    dve.wait_ge(S["acc"], m.i * ACC_STEPS + e)
                else:
                    dve.wait_ge(S["accinit"], m.i + 1)
                    dve.wait_ge(S["comb"], m.i + 1)
                for t in range(2):
                    last = dve.scalar_tensor_tensor(acc[:, m.b, t, :], p[:, t, :], comb[:, m.b, t, e:e + 1],
                                                    acc[:, m.b, t, :], ALU.mult, ALU.add)
                last.then_inc(S["acc"], 1)

            def body(g):
                cnt = Count(dve, S["link"], g.i * BODY_LINKS)
                here, before = g.within(0, NGR), g.within(1, NGR + 1)
                m = g.plus(-1)
                if here:
                    hidden_state(g, cnt)
                if before:
                    accumulate(m, 0)
                    accumulate(m, 1)
                if here:
                    mix_norm(g, cnt)
                    tokens(g, cnt)
                if before:
                    for e in range(2, NE + 1):
                        accumulate(m, e)
                if here:
                    route(g, cnt)
                    if isinstance(g.i, int):
                        assert cnt.at == (g.i + 1) * BODY_LINKS, cnt.at - g.i * BODY_LINKS

            dve.wait_ge(S["wrT_psum"], 1)
            dve.tensor_copy(wrT[:, :, :], pl[:, 0:KC * NE].rearrange("p (c e) -> p c e", c=KC)).then_inc(S["wrT"], 1)
            dve.wait_ge(s_c, 16 * NSMALL)
            group_bodies(dve, body, 1)

        @block.scalar
        def _(act):
            act.wait_ge(s_c, 16 * NSMALL)

            def body(g):
                here, before = g.within(0, NGR), g.within(1, NGR + 1)
                m = g.plus(-1)
                hid = Count(act, S["gelu"], hidden_base(g))

                def turned(src, dst, psum, made):
                    act.wait_ge(S[psum], g.i + 1)
                    act.activation(dst, src[:, 0:4 * P].rearrange("p (c n) -> p c n", c=KC), ACT.Copy).then_inc(S[made], 1)

                def gelu(dst, bias):
                    act.wait_ge(S["hidden"], hid.at + 1)
                    hid.mark(act.activation(dst, ph[hid_b[0] % 2][:, 0:2 * P], ACT.Gelu, bias=bias))
                    hid_b[0] += 1

                hid_b = [0]

                def expert(e):
                    y = m.i * (NE + 1) + e
                    wait(act, S["y"], y - 1)
                    for f in range(KC):
                        gelu(eT[:, e % 2, f, :], be1[:, e, f:f + 1])

                if here:
                    turned(pT[0], qT[:, :, :], "qT_psum", "qT")
                if before:
                    expert(0)
                    expert(1)
                if here:
                    turned(pT[1], hT[:, :, :], "hT_psum", "hT")
                    wait(act, S["ffn"], g.i)
                    for f in range(NF):
                        gelu(fT[:, f, :], bf1[:, f:f + 1])
                if before:
                    act.wait_ge(S["combT_psum"], m.i + 1)
                    wait(act, S["y"], m.i * (NE + 1))
                    act.activation(combT[:, :], pl[0:NE, 2 * P:4 * P], ACT.Copy).then_inc(S["combT"], 1)
                    for e in range(2, NE):
                        expert(e)
                if here:
                    turned(pT[0], tokT[:, g.b, :, :], "tokT_psum", "tokT")
                    act.wait_ge(S["logit_shift"], g.i + 1)
                    act.activation(pr[:, :, :], pr[:, :, :], ACT.Exp).then_inc(S["logit_exp"], 1)

            group_bodies(act, body, 1)

        @block.tensor
        def _(pe):
            pe.wait_ge(s_c, 16 * NSMALL)
            for cc in range(KC):
                t = pe.transpose(pl[:, cc * NE:(cc + 1) * NE], wr[:, cc * 128:(cc + 1) * 128], c.ident[0:NE, 0:NE])
            t.then_inc(S["wrT_psum"], 1)
            pe.wait_ge(s_w, 16 * (2 + 2 * NE))
            pe.wait_ge(S["wrT"], 1)

            def body(g):
                here, before = g.within(0, NGR), g.within(1, NGR + 1)
                m = g.plus(-1)
                hid = Count(pe, S["hidden"], hidden_base(g))
                hid_b = [0]

                def turn(dst, src, made):
                    for cc in range(KC):
                        for t in range(2):
                            x = pe.transpose(dst[:, (cc * 2 + t) * P:(cc * 2 + t + 1) * P],
                                             src[:, t, cc * 128:(cc + 1) * 128], c.ident[0:P, 0:P])
                    x.then_inc(S[made], 1)

                def hidden(weights, acts):
                    wait(pe, S["gelu"], hid.at - 1)
                    for cc in range(KC):
                        x = pe.matmul(ph[hid_b[0] % 2][:, 0:2 * P], weights(cc), acts[:, cc, :],
                                      start=cc == 0, stop=cc == KC - 1)
                    hid.mark(x)
                    hid_b[0] += 1

                def expert_up(e):
                    for f in range(KC):
                        hidden(lambda cc: We1[:, e, cc, f * 128:(f + 1) * 128], tokT[:, m.b, :, :])

                def expert_down(e, gelus):
                    y = m.i * (NE + 1) + e
                    wait(pe, S["acc"], y - 1)
                    pe.wait_ge(S["gelu"], gelus)
                    for t in range(2):
                        for f in range(KC):
                            x = pe.matmul(py[(m.b + e) % 2][0:P, t * D:(t + 1) * D], eT[:, e % 2, f, t * P:(t + 1) * P],
                                          We2[:, e, f, :], start=f == 0, stop=f == KC - 1)
                    x.then_inc(S["y"], 1)

                if here:
                    pe.wait_ge(s_qm[g.b], 16 * g.turn + 16)
                    wait(pe, S["tokT"], g.i)
                    turn(pT[0], qm[:, g.b, :, :], "qT_psum")
                if before:
                    expert_up(0)
                    up0 = hid.at
                    pe.wait_ge(S["comb"], m.i + 1)
                    for t in range(2):
                        x = pe.transpose(pl[0:NE, (2 + t) * P:(3 + t) * P], comb[:, m.b, t, :], c.ident[0:P, 0:P])
                    x.then_inc(S["combT_psum"], 1)
                    expert_up(1)
                    up1 = hid.at
                    expert_down(0, up0)
                if here:
                    pe.wait_ge(S["qT"], g.i + 1)
                    wait(pe, S["r2"], g.i)
                    for t in range(2):
                        for cc in range(KC):
                            x = pe.matmul(pw[0:P, t * D:(t + 1) * D], qT[:, cc, t * P:(t + 1) * P], c.mixmat[:, cc, :],
                                          start=cc == 0, stop=cc == KC - 1)
                    x.then_inc(S["mixed"], 1)
                if before:
                    expert_down(1, up1)
                if here:
                    pe.wait_ge(S["h"], g.i + 1)
                    wait(pe, S["hT"], g.i)
                    turn(pT[1], h, "hT_psum")
                    pe.wait_ge(S["hT"], g.i + 1)
                    for f in range(NF):
                        hidden(lambda cc: W1[:, cc, f * 128:(f + 1) * 128], hT)
                    pe.wait_ge(S["mixn"], g.i + 1)
                    pe.wait_ge(S["gelu"], hid.at)
                    for t in range(2):
                        for f in range(NF):
                            x = pe.matmul(pw[0:P, t * D:(t + 1) * D], fT[:, f, t * P:(t + 1) * P], W2[:, f, :],
                                          start=f == 0, stop=f == NF - 1)
                    x.then_inc(S["ffn"], 1)
                if before:
                    expert_up(2)
                    for e in range(3, NE):
                        ups = hid.at
                        expert_up(e)
                        expert_down(e - 1, ups)
                    expert_down(NE - 1, hid.at)
                    pe.wait_ge(S["combT"], m.i + 1)
                    wait(pe, S["acc"], m.i * (NE + 1) + NE - 1)
                    for t in range(2):
                        x = pe.matmul(py[(m.b + NE) % 2][0:P, t * D:(t + 1) * D], combT[:, t * P:(t + 1) * P], be2[:, :],
                                      start=True, stop=True)
                    x.then_inc(S["y"], 1)
                if here:
                    pe.wait_ge(S["tok"], g.i + 1)
                    turn(pT[0], tok, "tokT_psum")
                    pe.wait_ge(S["tokT"], g.i + 1)
                    for t in range(2):
                        for cc in range(KC):
                            x = pe.matmul(pl[0:P, t * NE:(t + 1) * NE], tokT[:, g.b, cc, t * P:(t + 1) * P],
                                          wrT[:, cc, :], start=cc == 0, stop=cc == KC - 1)
                    x.then_inc(S["logits"], 1)

            group_bodies(pe, body, 1)


_INS = ['x', 'src', 'dst', 'L0_gnn_Wq', 'L0_gnn_bq', 'L0_gnn_Wk', 'L0_gnn_bk', 'L0_gnn_Wv', 'L0_gnn_bv',
        'L0_gnn_Wskip', 'L0_gnn_bskip', 'L0_gnn_ln1_g', 'L0_gnn_ln1_b', 'L0_gnn_W1', 'L0_gnn_b1', 'L0_gnn_W2',
        'L0_gnn_b2', 'L0_gnn_ln2_g', 'L0_gnn_ln2_b', 'L0_mix_Wqkv', 'L0_mix_Wout', 'L0_mix_gamma',
        'L0_ffn_router_w', 'L0_ffn_w1', 'L0_ffn_b1', 'L0_ffn_w2', 'L0_ffn_b2']


def build(nc, w, out):
    kv_d = nc.dram_tensor("kv_rows", (N, 2 * D), F32, kind="Internal").ap()
    s1_d = nc.dram_tensor("skip_rows", (N, D), F32, kind="Internal").ap()
    qm_d = nc.dram_tensor("mixq_rows", (N, D), F32, kind="Internal").ap()
    with ExitStack() as ctx:
        c = Consts(ctx, nc)
        constants(nc, c)
        node_phase(nc, c, w["x"], w, kv_d, s1_d, qm_d)
        with ExitStack() as ectx:
            st = Steps(ectx, nc)
            step_tables(nc, c, st, w["src"], w["dst"])
            edge_phase(nc, c, st, kv_d)
        dense_phase(nc, c, w, s1_d, qm_d, out)


def kernel(**inputs):
    import numpy as _np
    import concourse.bacc as _bacc
    from concourse import mybir as _mybir
    from concourse.bass_utils import run_bass_kernel_spmd as _run

    nc = _bacc.Bacc("TRN2", target_bir_lowering=False, num_devices=1)
    arrays, args = {}, {}
    for name in _INS:
        a = _np.ascontiguousarray(inputs[name])
        arrays[f"in_{name}_dram"] = a
        args[name] = nc.dram_tensor(f"in_{name}_dram", a.shape, _mybir.dt.from_np(a.dtype), kind="ExternalInput").ap()
    out = nc.dram_tensor("out_dram", (N, D), _mybir.dt.float32, kind="ExternalOutput").ap()
    build(nc, args, out)
    r = _run(nc, [arrays], core_ids=[0])
    return r.results[0]["out_dram"]
```

```python
import concourse.bass as bass
from concourse import mybir
from contextlib import ExitStack

F32 = mybir.dt.float32
BF16 = mybir.dt.bfloat16
I32 = mybir.dt.int32
ALU = mybir.AluOpType
ACT = mybir.ActivationFunctionType
AX = mybir.AxisListType.X

N, D = 6250, 256
E = 100000
P = 125
NT = N // P
EG = 2 * P
NG = E // EG
H, HD = 4, D // 4
MH, MD = 8, D // 8
FF = 4 * D
NE = 8
KC = D // 128
NF = FF // 128
NGR = NT // 2
NSMALL = 8
CAP = N + P
ETILES = 2 * N // P + NE
SPARE = NE
GC = 4
GP = NG // GC
SPC = 8
NCH = -(-(NG + NT - 1) // (3 * SPC)) * 3
NSTEP = NCH * SPC
T = 2 * SPC
R = H * T
VH = HD + 1
SLOT = H * VH
ROW = D + SLOT
RING = 3
NEG = -float(2 ** 100)
EPS = 1e-5


def ds(start, size):
    return bass.ds(start, size)


def wait(eng, sem, value):
    if isinstance(value, int) and value <= 0:
        return
    eng.wait_ge(sem, value)


class Count:

    def __init__(self, eng, sem, at=0):
        self.eng, self.sem, self.at = eng, sem, at

    def mark(self, ins):
        ins.then_inc(self.sem, 1)
        self.at = self.at + 1
        return self.at

    def chain(self, ins, between=()):
        self.mark(ins)
        next(iter(between), None)
        self.eng.wait_ge(self.sem, self.at)


def hold(dve, cell):
    dve.memset(cell, 0.0)


def constants(nc, c, used):
    with ExitStack() as ctx:
        s_set = nc.alloc_semaphore("const_set")
        used.append(s_set)
        block = ctx.enter_context(nc.Block())

        @block.gpsimd
        def _(pool):
            cnt = Count(pool, s_set)
            cnt.mark(pool.memset(c.ident[:, :], 0.0))
            cnt.mark(pool.iota(c.iota[:, :], pattern=[[1, 128]], base=0, channel_multiplier=0,
                               allow_small_or_imprecise_dtypes=True))
            pool.wait_ge(s_set, cnt.at)
            pool.affine_select(out=c.ident[:, :], in_=c.ident[:, :], compare_op=ALU.not_equal, fill=1.0,
                               base=0, pattern=[[-1, 128]], channel_multiplier=1)

        @block.vector
        def _(dve):
            dve.memset(c.slots[:, 0, 0:D], 0.0)
            dve.memset(c.slots[:, :, D:SLOT], 0.0)


class Consts:
    def __init__(self, ctx, nc):
        def sb(name, shape, dt=F32):
            return ctx.enter_context(nc.sbuf_tensor(name, shape, dt))
        self.ident = sb("ident", [128, 128])
        self.iota = sb("iota", [128, 128])
        self.slots = sb("slots", [P, NT + 1, SLOT])
        self.mixmat = sb("mixmat", [128, KC, D])


class Group:

    def __init__(self, k, off):
        self.k, self.off = k, off
        self.i, self.b, self.turn = 2 * k + off, off % 2, k + off // 2

    def plus(self, n):
        return Group(self.k, self.off + n)

    def within(self, low, high):
        return not isinstance(self.i, int) or low <= self.i < high


def group_bodies(eng, body, extra=0, first=3):
    for g in range(first):
        body(Group(0, g))
    with eng.Fori(first // 2, (NGR - 3) // 2) as k:
        body(Group(k, 1))
        body(Group(k, 2))
    for g in range(NGR - 2, NGR + extra):
        body(Group((NGR - 3) // 2, g - (NGR - 3)))


def node_phase(nc, c, used, x, w, kv_d, s1_d, qm_d):
    with ExitStack() as ctx:
        def sb(name, shape, dt=F32):
            return ctx.enter_context(nc.sbuf_tensor("n_" + name, shape, dt))

        def ps(name, shape=(128, 512)):
            return ctx.enter_context(nc.psum_tensor("n_" + name, list(shape), F32))

        def sem(name):
            used.append(nc.alloc_semaphore("n_" + name))
            return used[-1]

        wg = sb("wg", [128, KC, 4 * D])
        wm = sb("wm", [128, KC, 3 * D])
        wo = sb("wo", [128, KC, D])
        bias = sb("bias", [P, 4, D])
        kmix = sb("kmix", [P, NT, D])
        vmix = sb("vmix", [P, NT, KC, 129])
        xt = sb("xt", [P, 2, 2, D])
        xn = sb("xn", [P, 2, 2, D])
        xnb = sb("xnb", [P, 2, D])
        xnT = sb("xnT", [128, 2, KC, P])
        kv = sb("kv", [P, 2, ROW])
        s1 = sb("s1", [P, 2, D])
        eq = sb("eq", [P, 2, D])
        qm = sb("qm", [P, 2, D])
        st = sb("st", [P, 2, 6])
        mv = sb("mv", [P, 2, 2])
        rstd = sb("rstd", [P, 2])
        power = sb("power", [P, 2, 2])
        cell = sb("cell", [1, 1])
        hm = sb("hm", [P, 3, MH])
        rmax = sb("rmax", [P, D])
        mcol = sb("mcol", [128, KC])
        mrow = sb("mrow", [1, D])
        mb = sb("mb", [P, D])
        ek = sb("ek", [P, 2, D])
        rz = sb("rz", [128, KC])
        ones = sb("ones", [1, P])
        headmask = sb("headmask", [128, 128])
        cxn = sb("cxn", [128, KC, 128])
        cxT = sb("cxT", [128, KC, 128])
        pT = ps("pT")
        pqk, pvs, pmqk, pmv = ps("pqk"), ps("pvs"), ps("pmqk"), ps("pmv")
        pcx = [ps(f"pcx{k}") for k in range(KC)]

        s_w = sem("weights_in")
        s_b = sem("biases_in")
        s_x = [sem(f"x_in{b}") for b in range(2)]
        s_st, s_var, s_rstd, s_eps, s_pw = (sem(n) for n in ("stats", "variance", "rstd", "var_eps", "power_set"))
        s_zero, s_sm = sem("mask_zeroed"), sem("softmax_link")
        s_d = sem("context_link")
        s_xn = sem("xn_made")
        s_xnb = sem("xnb_made")
        s_T = sem("xnT_in_psum")
        s_Tc = sem("xnT_made")
        s_g = [sem(f"proj{g}_made") for g in range(4)]
        s_qk = sem("qk_taken")
        s_vs = sem("vs_taken")
        s_eqr = sem("mixq_shifted")
        s_eq = sem("mixq_exp")
        s_rs = sem("mixq_rsum")
        s_qm = sem("mixq_made")
        s_km = sem("mixk_kept")
        s_vm = sem("mixv_kept")
        s_rm = sem("rmax_made")
        s_kvo = [sem(f"kv_out{b}") for b in range(2)]
        s_s1o = [sem(f"s1_out{b}") for b in range(2)]
        s_qmo = [sem(f"qm_out{b}") for b in range(2)]
        s_one = sem("vones_set")
        s_mpe, s_mdve = sem("keymax_turned"), sem("keymax_reduced")
        s_ks, s_ek, s_cx = sem("key_shifted"), sem("key_exp"), sem("context_added")
        s_cn, s_cT, s_cTc = sem("ctx_scaled"), sem("ctx_product"), sem("ctx_kept")
        block = ctx.enter_context(nc.Block())

        last_k = NT // 2 - 1

        def tiles(eng, body):
            for b in range(2):
                body(0, b)
            with eng.Fori(1, last_k) as k:
                for b in range(2):
                    body(k, b)
            for b in range(2):
                body(last_k, b)

        @block.sync
        def _(sp):
            for k, name in enumerate(("Wq", "Wk", "Wv", "Wskip")):
                sp.dma_start(wg[:, :, k * D:(k + 1) * D],
                             w["L0_gnn_" + name].rearrange("(c p) n -> p c n", p=128)).then_inc(s_w, 16)
            sp.dma_start(wm[:, :, :], w["L0_mix_Wqkv"].rearrange("(c p) n -> p c n", p=128)).then_inc(s_w, 16)
            sp.dma_start(wo[:, :, :], w["L0_mix_Wout"].rearrange("(c p) n -> p c n", p=128)).then_inc(s_w, 16)

            def load(g):
                wait(sp, s_xn, 2 * (g.i - 1))
                sp.dma_start(xt[:, g.b, :, :],
                             x[ds(g.i * (2 * P), 2 * P), :].rearrange("(t p) d -> p t d", p=P)).then_inc(s_x[g.b], 16)

            def store_qm(n, b):
                sp.wait_ge(s_qm, n + 1)
                sp.dma_start(qm_d[ds(n * P, P), :], qm[:, b, :]).then_inc(s_qmo[b], 16)

            load(Group(0, 0))
            for k, name in enumerate(("bq", "bk", "bv", "bskip")):
                sp.dma_start(bias[:, k, :], w["L0_gnn_" + name].partition_broadcast(P)).then_inc(s_b, 16)
            load(Group(0, 1))

            def body(g):
                if g.within(0, NGR - 2):
                    load(g.plus(2))
                for j in range(2):
                    n = 2 * g.i + j
                    sp.wait_ge(s_qk, n + 1)
                    sp.wait_ge(s_vs, n + 1)
                    sp.dma_start(kv_d[ds(n * P, P), :], kv[:, j, :]).then_inc(s_kvo[j], 16)
                    sp.dma_start(s1_d[ds(n * P, P), :], s1[:, j, :]).then_inc(s_s1o[j], 16)
                    if j or g.within(1, NGR):
                        store_qm(n - 1, 1 - j)

            group_bodies(sp, body)
            store_qm(NT - 1, 1)
            for s in (s_kvo, s_s1o, s_qmo):
                for b in range(2):
                    sp.wait_ge(s[b], 16 * (NT // 2))

        @block.vector
        def _(dve):
            def variance(g):
                dve.wait_ge(s_x[g.b], 16 * g.turn + 16)
                for j in range(2):
                    dve.bn_stats(st[:, j, :], xt[:, g.b, j, :]).then_inc(s_st, 1)
                dve.wait_ge(s_st, 2 * g.i + 2)
                wait(dve, s_xn, 2 * g.i)
                hold(dve, cell[:, :])
                for j in range(2):
                    dve.bn_aggr(mv[:, j, :], st[:, j, :]).then_inc(s_var, 1)

            def normalise(g):
                dve.wait_ge(s_rstd, g.i + 1)
                if g.within(2, NGR):
                    dve.wait_ge(s_xnb, 2 * g.i - 2)
                    dve.wait_ge(s_T, 2 * g.i - 2)
                for j in range(2):
                    dve.tensor_scalar(xn[:, g.b, j, :], xt[:, g.b, j, :], mv[:, j, 0:1], rstd[:, j:j + 1],
                                      ALU.subtract, ALU.mult).then_inc(s_xn, 1)

            def mixq_sum(n, b):
                dve.wait_ge(s_eq, n + 1)
                dve.tensor_reduce(hm[:, 1, :], eq[:, b, :].rearrange("p (h d) -> p h d", h=MH), AX, ALU.add
                                  ).then_inc(s_sm, 1)
                dve.wait_ge(s_sm, 2 * n + 2)
                wait(dve, s_qm, n)
                dve.reciprocal(hm[:, 2, :], hm[:, 1, :]).then_inc(s_rs, 1)

            def tile(g, j):
                n = 2 * g.i + j
                dve.wait_ge(s_g[0], n + 1)
                dve.tensor_tensor(c.slots[:, ds(n + 1, 1), 0:D].rearrange("p a d -> p (a d)"),
                                  pqk[0:P, 0:D], bias[:, 0, :], ALU.add)
                wait(dve, s_kvo[j], 16 * g.i)
                dve.tensor_tensor(kv[:, j, 0:D], pqk[0:P, D:2 * D], bias[:, 1, :], ALU.add).then_inc(s_qk, 1)
                if j or g.within(1, NGR):
                    mixq_sum(n - 1, 1 - j)
                dve.wait_ge(s_g[1], n + 1)
                dve.tensor_tensor(kv[:, j, D:ROW].rearrange("p (h v) -> p h v", h=H)[:, :, 0:HD],
                                  pvs[0:P, 0:D].rearrange("p (h v) -> p h v", h=H),
                                  bias[:, 2, :].rearrange("p (h v) -> p h v", h=H), ALU.add)
                dve.wait_ge(s_xnb, n + 1)
                wait(dve, s_s1o[j], 16 * g.i)
                dve.tensor_tensor(s1[:, j, :], pvs[0:P, D:2 * D], xnb[:, j, :], ALU.add).then_inc(s_vs, 1)
                if j == 0 and g.within(0, NGR - 1):
                    variance(g.plus(1))
                dve.wait_ge(s_g[2], n + 1)
                q3 = pmqk[0:P, 0:D].rearrange("p (h d) -> p h d", h=MH)
                dve.tensor_reduce(hm[:, 0, :], q3, AX, ALU.max).then_inc(s_sm, 1)
                if j == 0 and not g.within(1, NGR):
                    dve.tensor_copy(rmax[:, :], pmqk[0:P, D:2 * D]).then_inc(s_rm, 1)
                else:
                    dve.wait_ge(s_rm, n)
                    dve.tensor_tensor(rmax[:, :], rmax[:, :], pmqk[0:P, D:2 * D], ALU.max).then_inc(s_rm, 1)
                dve.wait_ge(s_sm, 2 * n + 1)
                wait(dve, s_qm, n - 1)
                dve.tensor_tensor(eq[:, j, :].rearrange("p (h d) -> p h d", h=MH), q3,
                                  hm[:, 0, :].unsqueeze(2).broadcast_to([P, MH, MD]), ALU.subtract).then_inc(s_eqr, 1)
                if j == 0 and g.within(0, NGR - 1):
                    normalise(g.plus(1))

            dve.memset(ones[:, :], 1.0)
            dve.memset(kv[:, :, D:ROW], 1.0)
            dve.memset(headmask[:, :], 0.0).then_inc(s_zero, 1)
            dve.wait_ge(s_zero, 1)
            for k in range(128 // MD):
                dve.memset(headmask[k * MD:(k + 1) * MD, k * MD:(k + 1) * MD], 1.0)
            variance(Group(0, 0))
            normalise(Group(0, 0))
            dve.wait_ge(s_b, 64)

            def body(g):
                for j in range(2):
                    tile(g, j)

            group_bodies(dve, body)
            mixq_sum(NT - 1, 1)

            cnt = Count(dve, s_d)
            dve.wait_ge(s_mpe, 1)
            dve.tensor_reduce(mcol[:, :], pT[:, 0:2 * P].rearrange("p (c n) -> p c n", c=KC),
                              AX, ALU.max).then_inc(s_mdve, 1)
            dve.wait_ge(s_mpe, 2)
            dve.tensor_copy(mrow[:, :], pmv[0:1, 0:D]).then_inc(s_mdve, 1)
            dve.wait_ge(s_mpe, 3)
            cnt.chain(dve.tensor_copy(mb[:, :], pvs[0:P, 0:D]))

            def shift(k, b):
                n = 2 * k + b
                wait(dve, s_cx, n - 1 if not isinstance(k, int) or k else 0)
                dve.tensor_tensor(ek[:, b, :], kmix[:, ds(n, 1), :].rearrange("p a d -> p (a d)"), mb[:, :],
                                  ALU.subtract).then_inc(s_ks, 1)

            tiles(dve, shift)
            dve.wait_ge(s_cx, NT)
            for cc in range(KC):
                cnt.chain(dve.reciprocal(rz[:, cc:cc + 1], pcx[cc][:, 128:129]))
                cnt.chain(dve.tensor_scalar(cxn[:, cc, :], pcx[cc][:, 0:128], rz[:, cc:cc + 1], MD ** -0.5,
                                            ALU.mult, ALU.mult))
                dve.tensor_tensor(cxn[:, cc, :], cxn[:, cc, :], headmask[:, :], ALU.mult).then_inc(s_cn, 1)
            dve.wait_ge(s_cT, 1)
            dve.tensor_copy(cxT[:, :, :], pT[:, 0:256].rearrange("p (c n) -> p c n", c=KC)).then_inc(s_cTc, 1)
            dve.wait_ge(s_cT, 2)
            dve.tensor_copy(c.mixmat[:, :, :], pqk[:, :].rearrange("p (c n) -> p c n", c=KC)).then_inc(s_cTc, 1)

        @block.gpsimd
        def _(pool):
            pool.memset(power[:, 0, :], -0.5).then_inc(s_pw, 1)
            pool.memset(power[:, 1, :], EPS).then_inc(s_pw, 1)
            pool.memset(vmix[:, :, :, 128:129], 1.0).then_inc(s_one, 1)
            pool.wait_ge(s_pw, 2)
            pool.wait_ge(s_b, 64)

            def reciprocal_root(g):
                pool.wait_ge(s_var, 2 * g.i + 2)
                wait(pool, s_xn, 2 * g.i)
                pool.tensor_tensor(rstd[:, :], mv[:, :, 1], power[:, 1, :], ALU.add).then_inc(s_eps, 1)
                pool.wait_ge(s_eps, g.i + 1)
                pool.tensor_tensor(rstd[:, :], rstd[:, :], power[:, 0, :], ALU.pow).then_inc(s_rstd, 1)

            def with_bias(g, j):
                n = 2 * g.i + j
                pool.wait_ge(s_xn, n + 1)
                wait(pool, s_vs, n - 1)
                pool.tensor_tensor(xnb[:, j, :], xn[:, g.b, j, :], bias[:, 3, :], ALU.add).then_inc(s_xnb, 1)

            def mixq(n, j, turn):
                pool.wait_ge(s_rs, n + 1)
                wait(pool, s_qmo[j], 16 * turn)
                pool.tensor_tensor(qm[:, j, :].rearrange("p (h d) -> p h d", h=MH),
                                   eq[:, j, :].rearrange("p (h d) -> p h d", h=MH),
                                   hm[:, 2, :].unsqueeze(2).broadcast_to([P, MH, MD]), ALU.mult).then_inc(s_qm, 1)

            def body(g):
                if g.within(1, NGR):
                    mixq(2 * g.i - 1, 1, g.i - 1)
                with_bias(g, 1)
                if g.within(0, NGR - 1):
                    reciprocal_root(g.plus(1))
                mixq(2 * g.i, 0, g.i)
                if g.within(0, NGR - 1):
                    with_bias(g.plus(1), 0)

            reciprocal_root(Group(0, 0))
            pool.wait_ge(s_b, 64)
            with_bias(Group(0, 0), 0)
            group_bodies(pool, body)
            mixq(NT - 1, 1, NGR - 1)

        @block.scalar
        def _(act):
            def keep_turned(n, b):
                act.wait_ge(s_T, n + 1)
                wait(act, s_g[3], n - 1)
                act.activation(xnT[:, b, :, :], pT[:, 0:2 * P].rearrange("p (c n) -> p c n", c=KC),
                               ACT.Copy).then_inc(s_Tc, 1)

            def body(g):
                for j in range(2):
                    n = 2 * g.i + j
                    if j == 0 or g.within(0, NGR - 1):
                        keep_turned(n + 1, 1 - j)
                    act.wait_ge(s_eqr, n + 1)
                    act.activation(kmix[:, ds(n, 1), :].rearrange("p a d -> p (a d)"), pmqk[0:P, D:2 * D],
                                   ACT.Copy).then_inc(s_km, 1)
                    act.activation(eq[:, j, :], eq[:, j, :], ACT.Exp).then_inc(s_eq, 1)
                    act.wait_ge(s_g[3], n + 1)
                    act.activation(vmix[:, ds(n, 1), :, 0:128].rearrange("p a c d -> p (a c) d"),
                                   pmv[0:P, 0:D].rearrange("p (c d) -> p c d", c=KC), ACT.Copy).then_inc(s_vm, 1)

            keep_turned(0, 0)
            group_bodies(act, body)

            def keyexp(k, b):
                act.wait_ge(s_ks, 2 * k + b + 1)
                act.activation(ek[:, b, :], ek[:, b, :], ACT.Exp).then_inc(s_ek, 1)

            tiles(act, keyexp)

        @block.tensor
        def _(pe):
            def turn(g, j):
                n = 2 * g.i + j
                pe.wait_ge(s_xn, n + 1)
                wait(pe, s_Tc, n)
                for cc in range(KC):
                    t = pe.transpose(pT[:, cc * P:(cc + 1) * P], xn[:, g.b, j, cc * 128:(cc + 1) * 128],
                                     c.ident[0:P, 0:P])
                t.then_inc(s_T, 1)

            def project(n, b, g, out, weights, freed):
                for s in freed:
                    wait(pe, s, n)
                for cc in range(KC):
                    m = pe.matmul(out, xnT[:, b, cc, :], weights(cc), start=cc == 0, stop=cc == KC - 1)
                m.then_inc(s_g[g], 1)

            def body(g):
                for j in range(2):
                    n = 2 * g.i + j
                    pe.wait_ge(s_Tc, n + 1)
                    project(n, j, 0, pqk[0:P, :], lambda cc: wg[:, cc, 0:2 * D], [s_qk])
                    project(n, j, 1, pvs[0:P, :], lambda cc: wg[:, cc, 2 * D:4 * D], [s_vs])
                    if j == 0 or g.within(0, NGR - 1):
                        turn(g.plus(j), 1 - j)
                    project(n, j, 2, pmqk[0:P, :], lambda cc: wm[:, cc, 0:2 * D], [s_km])
                    project(n, j, 3, pmv[0:P, 0:D], lambda cc: wm[:, cc, 2 * D:3 * D], [s_vm])

            turn(Group(0, 0), 0)
            pe.wait_ge(s_w, 16 * 6)
            group_bodies(pe, body)

            pe.wait_ge(s_rm, NT)
            pe.wait_ge(s_Tc, NT)
            for cc in range(KC):
                t = pe.transpose(pT[:, cc * P:(cc + 1) * P], rmax[:, cc * 128:(cc + 1) * 128], c.ident[0:P, 0:P])
            t.then_inc(s_mpe, 1)
            pe.wait_ge(s_mdve, 1)
            pe.wait_ge(s_vm, NT)
            for cc in range(KC):
                t = pe.transpose(pmv[0:1, cc * 128:(cc + 1) * 128], mcol[:, cc:cc + 1], c.ident[:, :])
            t.then_inc(s_mpe, 1)
            pe.wait_ge(s_mdve, 2)
            pe.wait_ge(s_vs, NT)
            pe.matmul(pvs[0:P, 0:D], ones[:, :], mrow[:, :], start=True, stop=True).then_inc(s_mpe, 1)
            pe.wait_ge(s_one, 1)

            def context(k, b):
                n = 2 * k + b
                pe.wait_ge(s_ek, n + 1)
                for cc in range(KC):
                    m = pe.matmul(pcx[cc][:, 0:129], ek[:, b, cc * 128:(cc + 1) * 128],
                                  vmix[:, ds(n, 1), cc, :].rearrange("p a d -> p (a d)"),
                                  start=isinstance(k, int) and n == 0, stop=isinstance(k, int) and n == NT - 1)
                m.then_inc(s_cx, 1)

            tiles(pe, context)
            pe.wait_ge(s_cn, KC)
            for cc in range(KC):
                t = pe.transpose(pT[:, cc * 128:(cc + 1) * 128], cxn[:, cc, :], c.ident[:, :])
            t.then_inc(s_cT, 1)
            pe.wait_ge(s_cTc, 1)
            for cc in range(KC):
                m = pe.matmul(pqk[:, cc * D:(cc + 1) * D], cxT[:, cc, :], wo[:, cc, :], start=True, stop=True)
            m.then_inc(s_cT, 1)


class Chunk:

    def __init__(self, i, off):
        self.i, self.off = i, off
        self.c, self.ring, self.turn = RING * i + off, off % RING, i + off // RING

    def plus(self, k):
        return Chunk(self.i, self.off + k)

    def within(self, low, high):
        return not isinstance(self.c, int) or low <= self.c < high

    def place(self, s):
        return (self.off * SPC + s) % RING

    def step(self, s):
        k = self.plus(s // SPC)
        return (k, s % SPC) if k.within(0, NCH) else None


def chunk_bodies(eng, body):
    for c in range(-1, RING):
        body(Chunk(0, c))
    with eng.Fori(1, NCH // RING - 1) as i:
        for u in range(RING):
            body(Chunk(i, u))
    for c in range(NCH - RING, NCH + 2):
        body(Chunk(NCH // RING - 1, c - (NCH - RING)))


class Steps:

    def __init__(self, ctx, nc):
        def sb(name, shape, dt=F32):
            return ctx.enter_context(nc.sbuf_tensor("e_" + name, shape, dt))
        self.src = sb("src", [P, 2 * NSTEP], I32)
        self.row = sb("row", [P, 2 * NSTEP])
        self.breaks = sb("breaks", [P, 2, 2 * NSTEP], BF16)
        self.mask = sb("mask", [P, 2 * NSTEP], BF16)
        self.keep = sb("keep", [P, NSTEP])
        self.tile = sb("tile", [1, NSTEP], I32)


def step_tables(nc, c, st, src, dst):
    with ExitStack() as ctx:
        def sb(name, shape, dt=F32):
            return ctx.enter_context(nc.sbuf_tensor("t_" + name, shape, dt))

        def sem(name):
            return ctx.enter_context(nc.semaphore("t_" + name))

        raw = sb("raw", [GP, 4, GC, EG], I32)
        val = sb("val", [GP, 2, GC, EG])
        edge = sb("edge", [GP, 2, GC, EG], BF16)
        thr = sb("thr", [GP, NT - 1])
        ones = sb("ones", [GP, 128], BF16)
        steps = sb("steps", [128, NSTEP])
        le = sb("le", [GP, GC, NT - 1])
        gid = sb("gid", [GP, GC])
        last = sb("last", [GP, GC])
        past = sb("past", [GP, GC, NSTEP], BF16)
        gq = sb("gq", [128, NSTEP])
        nq = sb("nq", [128, NSTEP])
        pick = sb("pick", [GP, GC, NSTEP])
        pickb = sb("pickb", [GP, GC, NSTEP], BF16)
        m2 = sb("m2", [P, 2, 2 * NSTEP])
        ps = [ctx.enter_context(nc.psum_tensor(f"t_ps{k}", [128, 512], F32)) for k in range(8)]
        s_set, s_in, s_io = sem("set"), sem("in"), sem("iota")
        s_v, s_past, s_cnt, s_pick, s_got = sem("link"), sem("past"), sem("cnt"), sem("pick"), sem("got")
        block = ctx.enter_context(nc.Block())

        @block.gpsimd
        def _(pool):
            pool.iota(gid[:, :], pattern=[[GP, GC]], base=0, channel_multiplier=1,
                      allow_small_or_imprecise_dtypes=True).then_inc(s_io, 1)
            pool.iota(steps[:, :], pattern=[[1, NSTEP]], base=0, channel_multiplier=0,
                      allow_small_or_imprecise_dtypes=True).then_inc(s_io, 1)
            pool.iota(thr[:, :], pattern=[[P, NT - 1]], base=P, channel_multiplier=0,
                      allow_small_or_imprecise_dtypes=True).then_inc(s_io, 1)

        @block.sync
        def _(sp):
            groups = dst.rearrange("(c g e) -> g c e", g=GP, e=EG)
            rows = dst.rearrange("(g e) -> g e", e=EG)
            sp.dma_start(raw[:, 0, :, :], groups).then_inc(s_in, 16)
            sp.dma_start(raw[:, 1, :, :], src.rearrange("(c g e) -> g c e", g=GP, e=EG)).then_inc(s_in, 16)
            sp.wait_ge(s_set, 1)
            with nc.allow_non_contiguous_dma("one element of each group"):
                for cc in range(GC):
                    sp.dma_start(raw[:, 2, cc, 1:EG], groups[:, cc, 0:EG - 1]).then_inc(s_in, 16)
                    sp.dma_start(raw[:, 3, cc, 0:EG - 1], groups[:, cc, 1:EG]).then_inc(s_in, 16)
                    lo = 1 if cc == 0 else 0
                    hi = GP - 1 if cc == GC - 1 else GP
                    sp.dma_start(raw[lo:GP, 2, cc, 0:1], rows[cc * GP + lo - 1:cc * GP + GP - 1, EG - 1:EG]).then_inc(s_in, 16)
                    sp.dma_start(raw[0:hi, 3, cc, EG - 1:EG], rows[cc * GP + 1:cc * GP + hi + 1, 0:1]).then_inc(s_in, 16)

        @block.vector
        def _(dve):
            cnt = Count(dve, s_v)
            dve.memset(ones[:, :], 1.0)
            dve.memset(raw[0:1, 2, 0, 0:1], -1)
            dve.memset(raw[96:GP, 3, GC - 1, EG - 1:EG], -1).then_inc(s_set, 1)
            dve.wait_ge(s_in, 16 * (2 + 4 * GC))
            cnt.mark(dve.tensor_copy(val[:, 1, :, :], raw[:, 1, :, :]))
            cnt.mark(dve.tensor_tensor(edge[:, 0, :, :], raw[:, 0, :, :], raw[:, 2, :, :], ALU.not_equal))
            cnt.mark(dve.tensor_tensor(edge[:, 1, :, :], raw[:, 0, :, :], raw[:, 3, :, :], ALU.not_equal))
            cnt.chain(dve.tensor_copy(val[:, 0, :, :], raw[:, 0, :, :]))
            dve.wait_ge(s_io, 3)
            for cc in range(GC):
                at = cnt.mark(dve.tensor_scalar(le[:, cc, :], thr[:, :], val[:, 0, cc, EG - 1:EG], None, ALU.is_le))
            dve.wait_ge(s_v, at)
            cnt.chain(dve.tensor_reduce(last[:, :], le[:, :, :], AX, ALU.add))
            cnt.chain(dve.tensor_tensor(last[:, :], last[:, :], gid[:, :], ALU.add))
            for cc in range(GC):
                m = dve.tensor_scalar(past[:, cc, :], steps[0:GP, :], last[:, cc:cc + 1], None, ALU.is_gt)
            m.then_inc(s_past, 1)
            dve.wait_ge(s_cnt, 1)
            cnt.chain(dve.tensor_scalar(gq[:, :], ps[7][:, 0:NSTEP], float(NG - 1), None, ALU.min))
            cnt.chain(dve.tensor_tensor(nq[:, :], steps[:, :], gq[:, :], ALU.subtract))
            for cc in range(GC):
                m = dve.tensor_scalar(pick[:, cc, :], gq[0:GP, :], gid[:, cc:cc + 1], None, ALU.is_equal)
            m.then_inc(s_pick, 1)
            for cc in range(GC):
                m = dve.tensor_scalar(pickb[:, cc, :], gq[0:GP, :], gid[:, cc:cc + 1], None, ALU.is_equal)
            m.then_inc(s_pick, 1)

            def pair(x):
                return x.rearrange("p (q j) -> p q j", j=2)

            dve.wait_ge(s_got, 1)
            for j in range(2):
                dve.tensor_copy(pair(st.src[:, :])[:, :, j], ps[2 + j][0:P, 0:NSTEP])
                cnt.mark(dve.scalar_tensor_tensor(pair(st.row[:, :])[:, :, j], nq[0:P, :], -float(P),
                                                  ps[j][0:P, 0:NSTEP], ALU.mult, ALU.add))
            dve.wait_ge(s_got, 2)
            for j in range(2):
                for f in range(2):
                    dve.tensor_scalar(pair(st.breaks[:, f, :])[:, :, j], ps[4 + 2 * f + j][0:P, 0:NSTEP],
                                      NEG, None, ALU.mult)
            dve.wait_ge(s_v, cnt.at)
            cnt.mark(dve.tensor_scalar(m2[:, 0, :], st.row[:, :], 0.0, NEG, ALU.is_lt, ALU.mult))
            cnt.chain(dve.tensor_scalar(m2[:, 1, :], st.row[:, :], float(P - 1), NEG, ALU.is_gt, ALU.mult))
            dve.tensor_tensor(st.mask[:, :], m2[:, 0, :], m2[:, 1, :], ALU.add)
            cnt.chain(dve.tensor_scalar(nq[:, :], nq[:, :], float(NT - 1), None, ALU.min))
            dve.tensor_copy(st.tile[:, :], nq[0:1, :])
            dve.memset(st.keep[:, 0:1], 0.0)
            dve.tensor_tensor(st.keep[:, 1:NSTEP], nq[0:P, 1:NSTEP], nq[0:P, 0:NSTEP - 1], ALU.is_equal)

        @block.tensor
        def _(pe):
            pe.wait_ge(s_past, 1)
            for cc in range(GC):
                m = pe.matmul(ps[7][:, 0:NSTEP], ones[:, :], past[:, cc, :], start=cc == 0, stop=cc == GC - 1)
            m.then_inc(s_cnt, 1)
            pe.wait_ge(s_pick, 1)
            for a in range(4):
                if a == 2:
                    m.then_inc(s_got, 1)
                    pe.wait_ge(s_pick, 2)
                table, chosen = (val[:, a], pick) if a < 2 else (edge[:, a - 2], pickb)
                for j in range(2):
                    for cc in range(GC):
                        m = pe.matmul(ps[2 * a + j][0:P, 0:NSTEP], table[:, cc, j * P:(j + 1) * P], chosen[:, cc, :],
                                      start=cc == 0, stop=cc == GC - 1)
            m.then_inc(s_got, 1)


def edge_phase(nc, c, st, kv_d):
    with ExitStack() as ctx:
        def sb(name, shape, dt=F32):
            return ctx.enter_context(nc.sbuf_tensor("e_" + name, shape, dt))

        def ps(name):
            return ctx.enter_context(nc.psum_tensor("e_" + name, [128, 512], F32))

        def sem(name):
            return ctx.enter_context(nc.semaphore("e_" + name))

        kv = sb("kv", [P, RING, SPC, 2, ROW])
        idx = sb("idx", [P, RING, T], I32)
        oh = sb("oh", [P, RING, SPC, 2, P])
        ohT = sb("ohT", [P, 2, 2, P])
        prod = sb("prod", [P, 2, D])
        score = sb("score", [P, RING, H, T])
        masked = sb("masked", [P, H, T])
        marks = sb("marks", [P, 2, H, T])
        marksT = sb("marksT", [R, 2, P])
        mark_sum = sb("mark_sum", [R, 2])
        fwd = sb("fwd", [R, P])
        bwd = sb("bwd", [R, P])
        carry_in = sb("carry_in", [R, 2])
        seg = sb("seg", [R, P])
        ex = sb("ex", [P, RING, H, T])
        row = sb("rows", [1, 5, H, T + 1])
        before = sb("before", [1, H, T])
        fix = sb("fix", [1, 3, H])
        scale = sb("scale", [P, H])
        wv = sb("wv", [P, RING, 2, SLOT])
        pq = [ps(f"pq{b}") for b in range(2)]
        pa = [ps(f"pa{b}") for b in range(2)]
        pt = [ps(f"pt{b}") for b in range(2)]
        pS, pX = ps("pS"), ps("pX")
        ptv = [pt[b][0:P, 0:2 * P].rearrange("p (j n) -> p j n", j=2) for b in range(2)]
        scoreT = pS[0:R, 0:P]
        marksP = pS[0:R, P:3 * P].rearrange("p (f e) -> p f e", f=2)
        pR = pS[0:1, P:P + 5 * R]
        rows3 = pR[:, 0:3 * R].rearrange("p (a h t) -> p a h t", a=3, h=H)
        rowb = pR[:, 3 * R:4 * R].rearrange("p (h t) -> p h t", h=H)
        rowm = pR[:, 4 * R:5 * R].rearrange("p (h t) -> p h t", h=H)
        exT = pX[0:P, 0:R]
        cinT = [pS[0:R, 500 + k:501 + k] for k in range(2)]
        growT = pX[0:P, 136:136 + H]
        RF0, RF1, RFO, RB0, RB1 = range(5)
        RBO = RB0

        s_gath = [[sem(f"rows_in{r}_{s}") for s in range(SPC // 2)] for r in range(RING)]
        names = ("idx_staged", "gather_go", "onehot", "onehotT_psum", "onehotT", "query_rows", "prod", "scored",
                 "masked", "marks", "scoreT", "marksT", "fwd_own", "ends", "fwd_rows", "fwd_carry", "bwd_own",
                 "starts", "bwd_rows", "bwd_carry", "segmax", "shifted", "exped", "maxrow", "exT", "ex",
                 "fixarg", "fixexp", "fixrow", "fixcol", "scale", "rescaled", "weighted", "summed", "added", "link", "turn_go")
        S = {n: sem(n) for n in names}
        block = ctx.enter_context(nc.Block())

        @block.gpsimd
        def _(pool):
            def gather(k):
                for s in range(SPC):
                    free = (k.c - RING) * SPC + s + 1
                    if s == 0:
                        wait(pool, S["weighted"], free)
                        pool.tensor_copy(idx[:, k.ring, :], st.src[:, ds(k.c * T, T)]).then_inc(S["idx_staged"], 1)
                        pool.wait_ge(S["idx_staged"], k.c + 1)
                    else:
                        wait(pool, S["weighted"], free)
                    pool.sem_inc(S["gather_go"], 1)
                    for j in range(2):
                        pool.indirect_dma_start(
                            out=kv[:, k.ring, s, j, :], out_offset=None, in_=kv_d[:, :],
                            in_offset=bass.IndirectOffsetOnAxis(ap=idx[:, k.ring, 2 * s + j:2 * s + j + 1], axis=0)
                        ).then_inc(s_gath[k.ring][s // 2], 16)

            for k in range(RING):
                gather(Chunk(0, k))
            with pool.Fori(1, NCH // RING) as i:
                for u in range(RING):
                    gather(Chunk(i, u))

        @block.vector
        def _(dve):
            cnt = Count(dve, S["link"])
            for a in (RF0, RF1, RB0, RB1):
                cnt.mark(dve.memset(row[:, a, :, :], NEG))
            dve.wait_ge(S["link"], cnt.at)

            def onehot(k, s):
                wait(dve, S["summed"], (k.c - RING) * SPC + s + 1)
                dve.tensor_tensor(oh[:, k.ring, s, :, :], c.iota[0:P, 0:P].unsqueeze(1).broadcast_to([P, 2, P]),
                                  st.row[:, ds((k.c * SPC + s) * 2, 2)].unsqueeze(2).broadcast_to([P, 2, P]),
                                  ALU.is_equal).then_inc(S["onehot"], 1)

            def score_step(k, s):
                q = k.c * SPC + s
                dve.wait_ge(S["query_rows"], q + 1)
                dve.wait_ge(s_gath[k.ring][s // 2], 64 * k.turn + 64)
                wait(dve, S["scored"], q)
                dve.tensor_tensor(prod[:, :, :], pq[s % 2][0:P, :].rearrange("p (j d) -> p j d", j=2),
                                  kv[:, k.ring, s, :, 0:D], ALU.mult).then_inc(S["prod"], 1)

            def score_sum(k, s):
                q = k.c * SPC + s
                dve.wait_ge(S["prod"], q + 1)
                dve.tensor_reduce(score[:, k.ring, :, 2 * s:2 * s + 2].rearrange("p h j -> p j h"),
                                  prod[:, :, :].rearrange("p j (h d) -> p j h d", h=H), AX, ALU.add
                                  ).then_inc(S["scored"], 1)

            def add_step(k, s, n):
                q = k.c * SPC + s
                wait(dve, S["added"], q)
                slot = c.slots[:, ds(n, 1), :].rearrange("p a v -> p (a v)")
                if s == 0 and k.within(1, NCH):
                    dve.wait_ge(S["scale"], k.c)
                    dve.tensor_tensor(slot.rearrange("p (h v) -> p h v", h=H), slot.rearrange("p (h v) -> p h v", h=H),
                                      scale[:, :].unsqueeze(2).broadcast_to([P, H, VH]),
                                      ALU.mult).then_inc(S["rescaled"], 1)
                    dve.wait_ge(S["rescaled"], k.c)
                dve.wait_ge(S["summed"], q + 1)
                dve.scalar_tensor_tensor(slot, slot, st.keep[:, ds(q, 1)], pa[s % 2][0:P, 0:SLOT],
                                         ALU.mult, ALU.add).then_inc(S["added"], 1)

            def softmax_stage(k, s):
                if s == 0:
                    dve.wait_ge(S["scored"], (k.c + 1) * SPC)
                    wait(dve, S["scoreT"], k.c)
                    dve.tensor_tensor(masked[:, :, :], score[:, k.ring, :, :],
                                      st.mask[:, ds(k.c * T, T)].unsqueeze(1).broadcast_to([P, H, T]),
                                      ALU.add).then_inc(S["masked"], 1)
                if s == 2:
                    dve.wait_ge(S["marksT"], k.c + 1)
                    dve.tensor_tensor_scan(fwd[:, :], marksT[:, 0, :], scoreT, NEG, ALU.add, ALU.max
                                           ).then_inc(S["fwd_own"], 1)
                if s == 3:
                    dve.wait_ge(S["ends"], k.c + 1)
                    if k.within(1, NCH):
                        dve.wait_ge(S["fwd_rows"], 3 * k.c)
                        dve.tensor_copy(row[:, RF1, :, 0], row[:, RFO, :, T])
                    dve.tensor_copy(row[:, RF1, :, 1:T + 1], rows3[:, 0, :, :])
                    dve.tensor_copy(row[:, RB0, :, 0:T], rows3[:, 2, :, :])
                    dve.tensor_copy(row[:, RF0, :, 1:T + 1], rows3[:, 1, :, :]).then_inc(S["fwd_rows"], 1)
                    dve.wait_ge(S["fwd_rows"], 3 * k.c + 1)
                    dve.tensor_tensor_scan(flat(RFO), flat(RF0), flat(RF1), NEG, ALU.add, ALU.max
                                           ).then_inc(S["fwd_rows"], 1)
                    dve.wait_ge(S["fwd_rows"], 3 * k.c + 2)
                    dve.tensor_copy(before[:, :, :], row[:, RFO, :, 0:T]).then_inc(S["fwd_rows"], 1)
                if s == 4:
                    dve.wait_ge(S["fwd_carry"], k.c + 1)
                    dve.tensor_copy(carry_in[:, 0:1], cinT[0]).then_inc(S["segmax"], 1)
                    dve.wait_ge(S["segmax"], 4 * k.c + 1)
                    dve.tensor_tensor_scan(fwd[:, :], marksT[:, 0, :], scoreT, carry_in[:, 0:1], ALU.add, ALU.max
                                           ).then_inc(S["segmax"], 1)
                    dve.wait_ge(S["segmax"], 4 * k.c + 2)
                    dve.tensor_tensor_scan(bwd[:, ::-1], marksT[:, 1, ::-1], fwd[:, ::-1], NEG, ALU.add, ALU.max
                                           ).then_inc(S["bwd_own"], 1)
                if s == 5:
                    dve.wait_ge(S["starts"], k.c + 1)
                    dve.tensor_copy(row[:, RB1, :, 0:T], rowb).then_inc(S["bwd_rows"], 1)
                    dve.wait_ge(S["bwd_rows"], 3 * k.c + 1)
                    dve.tensor_tensor_scan(flat(RBO)[:, ::-1], flat(RB0)[:, ::-1], flat(RB1)[:, ::-1], NEG,
                                           ALU.add, ALU.max).then_inc(S["bwd_rows"], 1)
                    dve.wait_ge(S["bwd_rows"], 3 * k.c + 2)
                    dve.tensor_copy(before[:, :, :], row[:, RBO, :, 1:T + 1]).then_inc(S["bwd_rows"], 1)
                if s == 6:
                    dve.wait_ge(S["bwd_carry"], k.c + 1)
                    dve.tensor_copy(carry_in[:, 1:2], cinT[1]).then_inc(S["segmax"], 1)
                    dve.wait_ge(S["segmax"], 4 * k.c + 3)
                    dve.tensor_tensor_scan(bwd[:, ::-1], marksT[:, 1, ::-1], fwd[:, ::-1], carry_in[:, 1:2],
                                           ALU.add, ALU.max).then_inc(S["segmax"], 1)
                    dve.wait_ge(S["segmax"], 4 * k.c + 4)
                    wait(dve, S["exT"], k.c)
                    dve.tensor_tensor(seg[:, :], scoreT, bwd[:, :], ALU.subtract).then_inc(S["shifted"], 1)
                if s == 7:
                    dve.wait_ge(S["maxrow"], k.c + 1)
                    wait(dve, S["fixexp"], k.c)
                    dve.tensor_tensor(fix[:, 0, :], row[:, RF1, :, 0], rowm[:, :, 0],
                                      ALU.subtract).then_inc(S["link"], 1)
                    dve.wait_ge(S["link"], k.c + 5)
                    dve.scalar_tensor_tensor(fix[:, 1, :], marks[0:1, 0, :, 0], 0.0, fix[:, 0, :],
                                             ALU.is_equal, ALU.mult).then_inc(S["fixarg"], 1)

            def flat(a):
                return row[:, a, :, :].rearrange("p h t -> p (h t)")

            def rescale_row(k):
                dve.wait_ge(S["fixexp"], k.c + 1)
                dve.tensor_scalar(fix[:, 2, :], fix[:, 2, :], -1.0, None, ALU.add).then_inc(S["fixrow"], 1)

            def rescale_col(k):
                dve.wait_ge(S["fixcol"], k.c)
                dve.tensor_scalar(scale[:, :], growT, 1.0, None, ALU.add).then_inc(S["scale"], 1)

            def body(k):
                nxt, prv = k.plus(1), k.plus(-1)
                for s in range(SPC):
                    add = prv.step(s - 3)
                    if s == 1 and prv.within(1, NCH):
                        rescale_row(prv)
                    if nxt.step(s - 1):
                        score_step(*nxt.step(s - 1))
                    if nxt.step(s + 3):
                        onehot(*nxt.step(s + 3))
                    if add:
                        n = dve.value_load(st.tile[0:1, ds(add[0].c * SPC + add[1], 1)], min_val=0, max_val=NT - 1)
                    if nxt.step(s - 1):
                        score_sum(*nxt.step(s - 1))
                    if add:
                        add_step(*add, n)
                    if s == 2 and prv.within(1, NCH):
                        rescale_col(prv)
                    if k.within(0, NCH):
                        softmax_stage(k, s)

            for s in range(3):
                onehot(Chunk(0, 0), s)
            chunk_bodies(dve, body)

        @block.scalar
        def _(act):
            def weight(k, s):
                q = k.c * SPC + s
                act.wait_ge(S["ex"], k.c + 1)
                wait(act, S["summed"], q - RING + 1)
                w4 = wv[:, k.place(s), :, :].rearrange("p j (h v) -> p j h v", h=H)
                for j in range(2):
                    for h in range(H):
                        m = act.activation(w4[:, j, h, :], kv[:, k.ring, s, j, D + h * VH:D + (h + 1) * VH],
                                           ACT.Copy, scale=ex[:, k.ring, h, 2 * s + j:2 * s + j + 1])
                m.then_inc(S["weighted"], 1)

            def keep_onehotT(k, s):
                q = k.c * SPC + s
                act.wait_ge(S["onehotT_psum"], q + 1)
                wait(act, S["query_rows"], q - 1)
                act.activation(ohT[:, s % 2, :, :], ptv[s % 2], ACT.Copy).then_inc(S["onehotT"], 1)

            def softmax_stage(k, s):
                if s == 0:
                    wait(act, S["fixarg"], k.c)
                    wait(act, S["scoreT"], k.c)
                    act.activation(marks[:, :, :, :],
                                   st.breaks[:, :, ds(k.c * T, T)].unsqueeze(2).broadcast_to([P, 2, H, T]),
                                   ACT.Copy).then_inc(S["marks"], 1)
                if s == 1:
                    act.wait_ge(S["scoreT"], k.c + 1)
                    wait(act, S["shifted"], k.c)
                    for f in range(2):
                        m = act.activation(marksT[:, f, :], marksP[:, f, :], ACT.Copy,
                                           accum_out=mark_sum[:, f:f + 1])
                    m.then_inc(S["marksT"], 1)

            def softmax_exp(k):
                act.wait_ge(S["shifted"], k.c + 1)
                act.activation(seg[:, :], seg[:, :], ACT.Exp, scale=HD ** -0.5).then_inc(S["exped"], 1)

            def softmax_kept(k):
                act.wait_ge(S["exT"], k.c + 1)
                act.activation(ex[:, k.ring, :, :].rearrange("p h t -> p (h t)"), exT, ACT.Copy
                               ).then_inc(S["ex"], 1)
                act.wait_ge(S["fixarg"], k.c + 1)
                wait(act, S["fixcol"], k.c - 1)
                act.activation(fix[:, 2, :], fix[:, 1, :], ACT.Exp, scale=HD ** -0.5).then_inc(S["fixexp"], 1)

            def body(k):
                nxt, prv = k.plus(1), k.plus(-1)
                for s in range(SPC):
                    if nxt.step(s + 1):
                        keep_onehotT(*nxt.step(s + 1))
                    if prv.step(s - 1):
                        weight(*prv.step(s - 1))
                    if s == SPC - 1 and k.within(0, NCH):
                        softmax_exp(k)
                    if s == 0 and prv.within(0, NCH):
                        softmax_kept(prv)
                    if k.within(0, NCH):
                        softmax_stage(k, s)

            keep_onehotT(Chunk(0, 0), 0)
            chunk_bodies(act, body)

        @block.tensor
        def _(pe):
            def turn_onehot(k, s):
                q = k.c * SPC + s
                pe.wait_ge(S["onehot"], q + 1)
                wait(pe, S["onehotT"], q - 1)
                for j in range(2):
                    m = pe.transpose(ptv[s % 2][:, j, :], oh[:, k.ring, s, j, :], c.ident[0:P, 0:P])
                m.then_inc(S["onehotT_psum"], 1)

            def query_rows(k, s, n):
                q = k.c * SPC + s
                pe.wait_ge(S["onehotT"], q + 1)
                wait(pe, S["prod"], q - 1)
                for j in range(2):
                    m = pe.matmul(pq[s % 2][0:P, j * D:(j + 1) * D], ohT[:, s % 2, j, :],
                                  c.slots[:, ds(n + 1, 1), 0:D].rearrange("p a d -> p (a d)"), start=True, stop=True)
                m.then_inc(S["query_rows"], 1)

            def sum_step(k, s):
                q = k.c * SPC + s
                pe.wait_ge(S["weighted"], q + 1)
                wait(pe, S["added"], q - 1)
                for j in range(2):
                    m = pe.matmul(pa[s % 2][0:P, 0:SLOT], oh[:, k.ring, s, j, :], wv[:, k.place(s), j, :],
                                  start=j == 0, stop=j == 1)
                m.then_inc(S["summed"], 1)

            idR = c.ident[0:R, 0:R]

            def softmax_stage(k, s):
                if s == 1:
                    pe.wait_ge(S["masked"], k.c + 1)
                    pe.wait_ge(S["marks"], k.c + 1)
                    wait(pe, S["shifted"], k.c)
                    wait(pe, S["marksT"], k.c)
                    pe.sem_inc(S["turn_go"], 1)
                    pe.transpose(scoreT, masked[:, :, :].rearrange("p h t -> p (h t)"), c.ident[0:P, 0:P])
                    for f in range(2):
                        m = pe.transpose(marksP[:, f, :], marks[:, f, :, :].rearrange("p h t -> p (h t)"),
                                         c.ident[0:P, 0:P])
                    m.then_inc(S["scoreT"], 1)
                if s == 3:
                    pe.wait_ge(S["fwd_own"], k.c + 1)
                    pe.wait_ge(S["marksT"], k.c + 1)
                    pe.sem_inc(S["turn_go"], 1)
                    for a, col in enumerate((fwd[:, P - 1:P], mark_sum[:, 0:1], mark_sum[:, 1:2])):
                        m = pe.transpose(pR[:, a * R:(a + 1) * R], col, idR)
                    m.then_inc(S["ends"], 1)
                if s == 4:
                    pe.wait_ge(S["fwd_rows"], 3 * k.c + 3)
                    pe.sem_inc(S["turn_go"], 1)
                    pe.transpose(cinT[0], before[:, :, :].rearrange("p h t -> p (h t)"), c.ident[0:1, 0:1]).then_inc(S["fwd_carry"], 1)
                if s == 5:
                    pe.wait_ge(S["bwd_own"], k.c + 1)
                    pe.sem_inc(S["turn_go"], 1)
                    pe.transpose(pR[:, 3 * R:4 * R], bwd[:, 0:1], idR).then_inc(S["starts"], 1)
                if s == 6:
                    pe.wait_ge(S["bwd_rows"], 3 * k.c + 3)
                    pe.sem_inc(S["turn_go"], 1)
                    pe.transpose(cinT[1], before[:, :, :].rearrange("p h t -> p (h t)"), c.ident[0:1, 0:1]).then_inc(S["bwd_carry"], 1)
                if s == 7:
                    pe.wait_ge(S["shifted"], k.c + 1)
                    wait(pe, S["fixarg"], k.c)
                    pe.sem_inc(S["turn_go"], 1)
                    pe.transpose(pR[:, 4 * R:5 * R], bwd[:, 0:1], idR).then_inc(S["maxrow"], 1)

            def exp_back(k):
                pe.wait_ge(S["exped"], k.c + 1)
                wait(pe, S["ex"], k.c)
                pe.sem_inc(S["turn_go"], 1)
                pe.transpose(exT, seg[:, :], idR).then_inc(S["exT"], 1)

            def body(k):
                nxt, prv = k.plus(1), k.plus(-1)
                for s in range(SPC):
                    if nxt.within(0, NCH):
                        n = pe.value_load(st.tile[0:1, ds(nxt.c * SPC + s, 1)], min_val=0, max_val=NT - 1)
                    if nxt.step(s + 2):
                        turn_onehot(*nxt.step(s + 2))
                    if nxt.within(0, NCH):
                        query_rows(nxt, s, n)
                    if s == 0 and prv.within(0, NCH):
                        exp_back(prv)
                    if s == 2 and prv.within(1, NCH):
                        pe.wait_ge(S["fixrow"], prv.c)
                        wait(pe, S["scale"], prv.c - 1)
                        pe.matmul(growT, oh[0:1, prv.ring, 0, 0, :], fix[:, 2, :], start=True, stop=True
                                  ).then_inc(S["fixcol"], 1)
                    if k.within(0, NCH):
                        softmax_stage(k, s)
                    if prv.step(s - 2):
                        sum_step(*prv.step(s - 2))

            for s in range(2):
                turn_onehot(Chunk(0, 0), s)
            chunk_bodies(pe, body)


class Routed:

    def __init__(self, ctx, nc):
        def sb(name, shape, dt=F32):
            return ctx.enter_context(nc.sbuf_tensor("x_" + name, shape, dt))
        self.We1, self.We2 = sb("We1", [128, NE, KC, D]), sb("We2", [128, NE, KC, D])
        self.be = sb("be", [P, 2, NE, D])
        self.share = sb("share", [P, NGR, 2, 2])
        self.choice = sb("choice", [P, NGR, 2, 2])
        self.place = sb("place", [P, NGR, 2, 2])
        self.result = sb("result", [P, NGR, 4], I32)
        self.placed = sb("placed", [P, NE])
        self.part = sb("part", [P, NE])
        self.zeros = sb("zeros", [P, D])
        self.loaded = ctx.enter_context(nc.semaphore("x_weights_in"))
        self.tok_d = nc.dram_tensor("token_rows", (NE * CAP + SPARE * P, D), F32, kind="Internal").ap()
        self.y_d = nc.dram_tensor("expert_rows", (ETILES * P, D), F32, kind="Internal").ap()
        self.base_d = nc.dram_tensor("base_rows", (N, D), F32, kind="Internal").ap()


def dense_phase(nc, c, xp, w, s1_d, qm_d):
    with ExitStack() as ctx:
        def sb(name, shape, dt=F32):
            return ctx.enter_context(nc.sbuf_tensor("d_" + name, shape, dt))

        def ps(name):
            return ctx.enter_context(nc.psum_tensor("d_" + name, [128, 512], F32))

        def sem(name):
            return ctx.enter_context(nc.semaphore("d_" + name))

        W1, W2 = sb("W1", [128, KC, FF]), sb("W2", [128, NF, D])
        bf1 = sb("bf1", [128, NF])
        wr, wrT = sb("wr", [NE, D]), sb("wrT", [128, KC, NE])
        rows = sb("rows", [P, 6, D])
        LG1, LB1, FB2, LG2, LB2, GAM = range(6)
        s1, qm, xt = (sb(n, [P, 2, 2, D]) for n in ("s1", "qm", "xt"))
        h, hb, tok, base = (sb(n, [P, 2, 2, D]) for n in ("h", "hb", "tok", "base"))
        r, rh, mix = (sb(n, [P, 2, D]) for n in ("r", "rh", "mix"))
        qT, hT, tokT = (sb(n, [128, KC, 2 * P]) for n in ("qT", "hT", "tokT"))
        fT = sb("fT", [128, NF, 2 * P])
        den = sb("den", [P, 2, 2, H])
        st, mv, rstd = sb("st", [P, 4, 2, 6]), sb("mv", [P, 4, 2, 2]), sb("rstd", [P, 4, 2])
        power = sb("power", [P, 2, 2])
        HIDDEN, MIX, FED, TOKEN = range(4)
        pr = sb("pr", [P, 2, NE])
        pm = sb("pm", [P, 4, 2])
        left = sb("left", [P, 2, NE])
        top = sb("top", [P, 2, 2])
        key = sb("key", [P, 2, NE])
        best = sb("best", [P, 2, 2])
        falling = sb("falling", [P, NE])
        hit = sb("hit", [P, 2, 2, NE])
        hits = sb("hits", [P, 2, NE])
        rank = sb("rank", [P, 2, NE])
        picked = sb("picked", [P, 2, 2, NE])
        placef = sb("placef", [P, 2, 2])
        idx = sb("idx", [P, 2, 4], I32)
        earlier = sb("earlier", [P, P])
        ones = sb("ones", [P, P])
        cell = sb("cell", [1, 1])
        ph = [ps(f"ph{b}") for b in range(2)]
        pT = [ps(f"pT{b}") for b in range(2)]
        pmix, pffn, pl, pk = ps("pmix"), ps("pffn"), ps("pl"), ps("pk")

        s_w, s_c = sem("weights_in"), sem("small_in")
        s_s1, s_qm, s_x, s_base, s_sent = ([sem(f"{n}{b}") for b in range(2)]
                                           for n in ("s1_in", "qm_in", "x_in", "base_out", "tokens_out"))
        names = ("set", "h", "h_link", "tok_link", "route_link", "hb", "mixn", "mixx", "r2", "mix_link", "tok", "base", "logit_shift",
                 "logit_exp", "qT_psum", "qT", "hT_psum", "hT", "tokT_psum", "tokT", "mixed", "ffn", "hidden", "gelu",
                 "logits", "wrT_psum", "wrT", "hits", "ranked", "place", "place_link", "go")
        S = {n: sem(n) for n in names}
        s_var = [sem(f"var{k}") for k in range(4)]
        s_rstd = [sem(f"rstd{k}") for k in range(4)]
        block = ctx.enter_context(nc.Block())

        def pair(x):
            return x[0:P, :].rearrange("p (t d) -> p t d", t=2)

        def bcast(k):
            return rows[:, k, :].unsqueeze(1).broadcast_to([P, 2, D])

        @block.sync
        def _(sp):
            def load(g):
                for dst, src, s, used, count in ((s1, s1_d, s_s1, "h", g.i - 1), (qm, qm_d, s_qm, "qT_psum", g.i - 1),
                                                 (xt, w["x"], s_x, "mixx", 2 * (g.i - 1))):
                    wait(sp, S[used], count)
                    sp.dma_start(dst[:, g.b, :, :],
                                 src[ds(g.i * (2 * P), 2 * P), :].rearrange("(t p) d -> p t d", p=P)).then_inc(s[g.b], 16)

            def store(g):
                sp.wait_ge(S["base"], g.i + 1)
                sp.dma_start(xp.base_d[ds(g.i * (2 * P), 2 * P), :].rearrange("(t p) d -> p t d", p=P),
                             base[:, g.b, :, :]).then_inc(s_base[g.b], 16)

            load(Group(0, 0))
            for k, name in enumerate(("ln1_g", "ln1_b", "b2", "ln2_g", "ln2_b")):
                sp.dma_start(rows[:, k, :], w["L0_gnn_" + name].partition_broadcast(P)).then_inc(s_c, 16)
            sp.dma_start(rows[:, GAM, :], w["L0_mix_gamma"].partition_broadcast(P)).then_inc(s_c, 16)
            sp.dma_start(wr[:, :], w["L0_ffn_router_w"]).then_inc(s_c, 16)
            with nc.allow_non_contiguous_dma("biases by column, a few KB"):
                sp.dma_start(bf1[:, :], w["L0_gnn_b1"].rearrange("(f p) -> p f", p=128)).then_inc(s_c, 16)
            load(Group(0, 1))
            sp.dma_start(W1[:, :, :], w["L0_gnn_W1"].rearrange("(c p) n -> p c n", p=128)).then_inc(s_w, 16)
            sp.dma_start(W2[:, :, :], w["L0_gnn_W2"].rearrange("(c p) n -> p c n", p=128)).then_inc(s_w, 16)
            for e in range(NE):
                sp.dma_start(xp.We1[:, e, :, :], w["L0_ffn_w1"][e, :, :].rearrange("(c p) n -> p c n", p=128)).then_inc(xp.loaded, 16)
                sp.dma_start(xp.We2[:, e, :, :], w["L0_ffn_w2"][e, :, :].rearrange("(c p) n -> p c n", p=128)).then_inc(xp.loaded, 16)
                for k, name in enumerate(("b1", "b2")):
                    sp.dma_start(xp.be[:, k, e, :], w["L0_ffn_" + name][e, :].partition_broadcast(P)).then_inc(xp.loaded, 16)

            def body(g):
                if g.within(0, NGR - 2):
                    load(g.plus(2))
                if g.within(1, NGR + 1):
                    store(g.plus(-1))

            group_bodies(sp, body, 2, 5)
            for b in range(2):
                sp.wait_ge(s_base[b], 16 * ((NGR + 1 - b) // 2))

        @block.gpsimd
        def _(pool):
            pool.memset(power[:, 0, :], -0.5).then_inc(S["set"], 1)
            pool.memset(power[:, 1, :], EPS).then_inc(S["set"], 1)
            pool.memset(ones[:, :], 1.0).then_inc(S["set"], 1)
            pool.iota(xp.part[:, :], pattern=[[CAP, NE]], base=0, channel_multiplier=0,
                      allow_small_or_imprecise_dtypes=True).then_inc(S["set"], 1)
            pool.iota(falling[:, :], pattern=[[-1, NE]], base=NE, channel_multiplier=0,
                      allow_small_or_imprecise_dtypes=True).then_inc(S["set"], 1)
            pool.wait_ge(S["set"], 5)
            pool.affine_select(out=earlier[:, :], in_=ones[:, :], compare_op=ALU.is_gt, fill=0.0,
                               base=0, pattern=[[1, P]], channel_multiplier=-1).then_inc(S["set"], 1)
            pool.wait_ge(s_c, 16 * NSMALL)

            def reciprocal_root(g, which):
                pool.wait_ge(s_var[which], g.i + 1)
                pool.tensor_tensor(rstd[:, which, :], mv[:, which, :, 1], power[:, 1, :], ALU.add
                                   ).then_inc(s_rstd[which], 1)
                pool.wait_ge(s_rstd[which], 2 * g.i + 1)
                pool.tensor_tensor(rstd[:, which, :], rstd[:, which, :], power[:, 0, :], ALU.pow
                                   ).then_inc(s_rstd[which], 1)

            def hidden_bias(g):
                pool.wait_ge(S["h"], g.i + 1)
                wait(pool, S["r2"], g.i - 1)
                pool.tensor_tensor(hb[:, g.b, :, :], h[:, g.b, :, :], bcast(FB2), ALU.add).then_inc(S["hb"], 1)

            def body(g):
                here, nxt, prv, old = g.within(0, NGR), g.within(-1, NGR - 1), g.within(1, NGR + 1), g.within(2, NGR + 2)
                if prv:
                    reciprocal_root(g.plus(-1), FED)
                if nxt:
                    reciprocal_root(g.plus(1), HIDDEN)
                if prv:
                    reciprocal_root(g.plus(-1), TOKEN)
                if nxt:
                    hidden_bias(g.plus(1))
                if here:
                    reciprocal_root(g, MIX)
                if prv:
                    m = g.plus(-1)
                    pool.wait_ge(S["tok"], m.i + 1)
                    if m.within(2, NGR):
                        pool.wait_ge(s_base[m.b], 16 * m.turn)
                    pool.tensor_tensor(base[:, m.b, :, :], r[:, :, :], tok[:, m.b, :, :], ALU.add).then_inc(S["base"], 1)
                if here:
                    pool.wait_ge(S["mixn"], g.i + 1)
                    pool.tensor_tensor(mix[:, :, :], mix[:, :, :], bcast(GAM), ALU.mult).then_inc(S["mixx"], 1)
                    pool.wait_ge(S["mixx"], 2 * g.i + 1)
                    pool.wait_ge(s_x[g.b], 16 * g.turn + 16)
                    pool.tensor_tensor(mix[:, :, :], mix[:, :, :], xt[:, g.b, :, :], ALU.add).then_inc(S["mixx"], 1)
                if old:
                    m = g.plus(-2)
                    pool.wait_ge(S["place"], m.i + 1)
                    pool.sem_inc(S["go"], 1)
                    for k in range(2):
                        for t in range(2):
                            pool.indirect_dma_start(
                                out=xp.tok_d[:, :],
                                out_offset=bass.IndirectOffsetOnAxis(ap=idx[:, m.b, 2 * k + t:2 * k + t + 1], axis=0),
                                in_=tok[:, m.b, t, :], in_offset=None).then_inc(s_sent[m.b], 16)

            reciprocal_root(Group(0, 0), HIDDEN)
            hidden_bias(Group(0, 0))
            group_bodies(pool, body, 2, 5)
            for b in range(2):
                pool.wait_ge(s_sent[b], 64 * ((NGR + 1 - b) // 2))

        @block.vector
        def _(dve):
            def variance(g, which, src, link, at, other=()):
                for t in range(2):
                    m = dve.bn_stats(st[:, which, t, :], src[:, t, :])
                m.then_inc(link, 1)
                next(iter(other), None)
                dve.wait_ge(link, at + 1)
                hold(dve, cell[:, :])
                for t in range(2):
                    m = dve.bn_aggr(mv[:, which, t, :], st[:, which, t, :])
                m.then_inc(s_var[which], 1)

            def normalised(g, which, src, dst, done):
                dve.wait_ge(s_rstd[which], 2 * g.i + 2)
                for t in range(2):
                    m = dve.tensor_scalar(dst[:, t, :], src[:, t, :], mv[:, which, t, 0:1],
                                          rstd[:, which, t:t + 1], ALU.subtract, ALU.mult)
                m.then_inc(done, 1)

            HL, TL, RL, PL = 7, 6, 18, 3

            def hidden_1(g, other=()):
                cnt = Count(dve, S["h_link"], g.i * HL)
                slot = c.slots[:, ds(2 * g.i, 2), :].rearrange("p t (h v) -> p t h v", h=H)
                cnt.chain(dve.tensor_scalar(den[:, 0, :, :], slot[:, :, :, HD], 1e-16, None, ALU.add), other)
                cnt.chain(dve.reciprocal(den[:, 1, :, :], den[:, 0, :, :]), other)
                r4 = rh[:, :, :].rearrange("p t (h v) -> p t h v", h=H)
                for t in range(2):
                    m = dve.tensor_tensor(r4[:, t], slot[:, t, :, 0:HD],
                                          den[:, 1, t, :].unsqueeze(2).broadcast_to([P, H, HD]), ALU.mult)
                cnt.chain(m, other)
                dve.wait_ge(s_s1[g.b], 16 * g.turn + 16)
                cnt.chain(dve.tensor_tensor(rh[:, :, :], rh[:, :, :], s1[:, g.b, :, :], ALU.add), other)
                variance(g, HIDDEN, rh, S["h_link"], cnt.at, other)

            def hidden_2(g):
                cnt = Count(dve, S["h_link"], g.i * HL + 5)
                wait(dve, S["hT_psum"], g.i - 1)
                wait(dve, S["hb"], g.i - 1)
                normalised(g, HIDDEN, rh, h[:, g.b, :, :], S["h_link"])
                cnt.at = cnt.at + 1
                dve.wait_ge(S["h_link"], cnt.at)
                cnt.chain(dve.tensor_tensor(h[:, g.b, :, :], h[:, g.b, :, :], bcast(LG1), ALU.mult))
                dve.tensor_tensor(h[:, g.b, :, :], h[:, g.b, :, :], bcast(LB1), ALU.add).then_inc(S["h"], 1)

            def tokens_1(g, other=()):
                dve.wait_ge(S["ffn"], g.i + 1)
                wait(dve, S["base"], g.i)
                dve.wait_ge(S["hb"], g.i + 1)
                dve.tensor_tensor(r[:, :, :], pair(pffn), hb[:, g.b, :, :], ALU.add).then_inc(S["r2"], 1)
                next(iter(other), None)
                dve.wait_ge(S["r2"], g.i + 1)
                variance(g, FED, r, S["tok_link"], g.i * TL, other)

            def tokens_2(g, other=()):
                cnt = Count(dve, S["tok_link"], g.i * TL + 1)
                normalised(g, FED, r, r, S["tok_link"])
                cnt.at = cnt.at + 1
                next(iter(other), None)
                dve.wait_ge(S["tok_link"], cnt.at)
                cnt.chain(dve.tensor_tensor(r[:, :, :], r[:, :, :], bcast(LG2), ALU.mult), other)
                cnt.chain(dve.tensor_tensor(r[:, :, :], r[:, :, :], bcast(LB2), ALU.add), other)
                dve.wait_ge(S["mixx"], 2 * g.i + 2)
                cnt.chain(dve.tensor_tensor(r[:, :, :], r[:, :, :], mix[:, :, :], ALU.add), other)
                variance(g, TOKEN, r, S["tok_link"], cnt.at, other)

            def tokens_3(g):
                wait(dve, S["tokT_psum"], g.i - 1)
                if g.within(2, NGR):
                    dve.wait_ge(s_sent[g.b], 64 * g.turn)
                normalised(g, TOKEN, r, tok[:, g.b, :, :], S["tok"])

            def mix_1(g):
                dve.wait_ge(S["mixed"], g.i + 1)
                for t in range(2):
                    m = dve.bn_stats(st[:, MIX, t, :], pair(pmix)[:, t, :])
                m.then_inc(S["mix_link"], 1)
                dve.wait_ge(S["mix_link"], g.i + 1)
                hold(dve, cell[:, :])
                for t in range(2):
                    m = dve.bn_aggr(mv[:, MIX, t, :], st[:, MIX, t, :])
                m.then_inc(s_var[MIX], 1)

            def mix_2(g):
                normalised(g, MIX, pair(pmix), mix, S["mixn"])

            def route(g):
                cnt = Count(dve, S["route_link"], g.i * RL)
                lg = pl[0:P, 0:2 * NE].rearrange("p (t e) -> p t e", t=2)
                dve.wait_ge(S["logits"], g.i + 1)
                cnt.chain(dve.tensor_reduce(pm[:, 0, :], lg, AX, ALU.max))
                dve.tensor_tensor(pr[:, :, :], lg, pm[:, 0, :].unsqueeze(2).broadcast_to([P, 2, NE]),
                                  ALU.subtract).then_inc(S["logit_shift"], 1)

            def choose(g):
                cnt = Count(dve, S["route_link"], g.i * RL + 1)
                dve.wait_ge(S["logit_exp"], g.i + 1)
                cnt.mark(dve.tensor_reduce(pm[:, 1, :], pr[:, :, :], AX, ALU.add))
                yield
                dve.wait_ge(S["route_link"], cnt.at)
                cnt.mark(dve.reciprocal(pm[:, 2, :], pm[:, 1, :]))
                yield
                dve.wait_ge(S["route_link"], cnt.at)
                cnt.mark(dve.tensor_tensor(pr[:, :, :], pr[:, :, :],
                                            pm[:, 2, :].unsqueeze(2).broadcast_to([P, 2, NE]), ALU.mult))
                yield
                dve.wait_ge(S["route_link"], cnt.at)
                wait(dve, S["place"], g.i)
                for k, p in enumerate((pr, left)):
                    cnt.mark(dve.tensor_reduce(top[:, k, :], p[:, :, :], AX, ALU.max))
                    yield
                    dve.wait_ge(S["route_link"], cnt.at)
                    cnt.mark(dve.tensor_tensor(key[:, :, :], p[:, :, :], top[:, k, :].unsqueeze(2).broadcast_to([P, 2, NE]),
                                                ALU.is_equal))
                    yield
                    dve.wait_ge(S["route_link"], cnt.at)
                    cnt.mark(dve.tensor_tensor(key[:, :, :], key[:, :, :],
                                                falling[:, :].unsqueeze(1).broadcast_to([P, 2, NE]), ALU.mult))
                    yield
                    dve.wait_ge(S["route_link"], cnt.at)
                    cnt.mark(dve.tensor_reduce(best[:, k, :], key[:, :, :], AX, ALU.max))
                    yield
                    dve.wait_ge(S["route_link"], cnt.at)
                    cnt.mark(dve.tensor_tensor(hit[:, k, :, :], key[:, :, :],
                                                best[:, k, :].unsqueeze(2).broadcast_to([P, 2, NE]), ALU.is_equal))
                    yield
                    dve.wait_ge(S["route_link"], cnt.at)
                    if k == 0:
                        cnt.mark(dve.scalar_tensor_tensor(left[:, :, :], hit[:, 0, :, :], -2.0, pr[:, :, :],
                                                           ALU.mult, ALU.add))
                        yield
                        dve.wait_ge(S["route_link"], cnt.at)
                dve.tensor_tensor(hits[:, :, :], hit[:, 0, :, :], hit[:, 1, :, :], ALU.add).then_inc(S["hits"], 1)
                cnt.mark(dve.tensor_tensor(pm[:, 3, :], top[:, 0, :], top[:, 1, :], ALU.add))
                yield
                dve.wait_ge(S["route_link"], cnt.at)
                dve.tensor_scalar(xp.choice[:, ds(g.i, 1), :, :].rearrange("p a k t -> p (a k) t"), best[:, :, :],
                                  -1.0, float(NE), ALU.mult, ALU.add)
                cnt.mark(dve.tensor_scalar(pm[:, 3, :], pm[:, 3, :], 1e-12, None, ALU.max))
                yield
                dve.wait_ge(S["route_link"], cnt.at)
                cnt.mark(dve.reciprocal(pm[:, 2, :], pm[:, 3, :]))
                yield
                dve.wait_ge(S["route_link"], cnt.at)
                dve.tensor_tensor(xp.share[:, ds(g.i, 1), :, :].rearrange("p a k t -> p (a k) t"), top[:, :, :],
                                  pm[:, 2, :].unsqueeze(1).broadcast_to([P, 2, 2]), ALU.mult)
                if isinstance(g.i, int):
                    assert cnt.at == (g.i + 1) * RL, cnt.at - g.i * RL

            def places(g):
                cnt = Count(dve, S["place_link"], g.i * PL)
                dve.wait_ge(S["ranked"], g.i + 1)
                cnt.mark(dve.tensor_tensor(rank[:, :, :], pk[0:P, 0:2 * NE].rearrange("p (t e) -> p t e", t=2),
                                           xp.placed[:, :].unsqueeze(1).broadcast_to([P, 2, NE]), ALU.add))
                dve.wait_ge(S["place_link"], cnt.at)
                dve.tensor_tensor(xp.placed[:, :], xp.placed[:, :], pk[0:P, 2 * NE:3 * NE], ALU.add)
                for k in range(2):
                    m = dve.tensor_tensor(picked[:, k, :, :], rank[:, :, :], hit[:, k, :, :], ALU.mult)
                cnt.mark(m)
                dve.wait_ge(S["place_link"], cnt.at)
                cnt.chain(dve.tensor_reduce(placef[:, :, :], picked[:, :, :, :], AX, ALU.add))
                if g.within(2, NGR):
                    dve.wait_ge(s_sent[g.b], 64 * g.turn)
                dve.tensor_copy(idx[:, g.b, :], placef[:, :, :].rearrange("p k t -> p (k t)"))
                dve.tensor_copy(xp.place[:, ds(g.i, 1), :, :].rearrange("p a k t -> p (a k) t"), placef[:, :, :]
                                ).then_inc(S["place"], 1)

            def body(g):
                here, nxt, prv, old = g.within(0, NGR), g.within(-1, NGR - 1), g.within(1, NGR + 1), g.within(2, NGR + 2)
                other = choose(g.plus(-2)) if old else iter(())
                if prv:
                    tokens_1(g.plus(-1), other)
                if nxt:
                    hidden_1(g.plus(1), other)
                if prv:
                    tokens_2(g.plus(-1), other)
                for _ in other:
                    pass
                if prv:
                    tokens_3(g.plus(-1))
                if nxt:
                    hidden_2(g.plus(1))
                if here:
                    mix_1(g)
                if old:
                    places(g.plus(-2))
                if here:
                    mix_2(g)
                if prv:
                    route(g.plus(-1))

            dve.wait_ge(S["wrT_psum"], 1)
            dve.tensor_copy(wrT[:, :, :], pl[:, 0:KC * NE].rearrange("p (c e) -> p c e", c=KC)).then_inc(S["wrT"], 1)
            dve.wait_ge(S["set"], 5)
            dve.tensor_copy(xp.placed[:, :], xp.part[:, :])
            dve.memset(xp.zeros[:, :], 0.0)
            dve.wait_ge(s_c, 16 * NSMALL)
            hidden_1(Group(0, 0))
            hidden_2(Group(0, 0))
            group_bodies(dve, body, 2, 5)

        @block.scalar
        def _(act):
            act.wait_ge(s_c, 16 * NSMALL)

            def turned(g, src, dst, psum, made, used):
                act.wait_ge(S[psum], g.i + 1)
                wait(act, S[used], g.i)
                act.activation(dst, src[:, 0:4 * P].rearrange("p (c n) -> p c n", c=KC), ACT.Copy).then_inc(S[made], 1)

            def body(g):
                here, prv = g.within(0, NGR), g.within(1, NGR + 1)
                if here:
                    turned(g, pT[0], qT[:, :, :], "qT_psum", "qT", "mixed")
                    turned(g, pT[1], hT[:, :, :], "hT_psum", "hT", "ffn")
                    for f in range(NF):
                        act.wait_ge(S["hidden"], g.i * NF + f + 1)
                        act.activation(fT[:, f, :], ph[f % 2][:, 0:2 * P], ACT.Gelu, bias=bf1[:, f:f + 1]
                                       ).then_inc(S["gelu"], 1)
                if prv:
                    m = g.plus(-1)
                    turned(m, pT[0], tokT[:, :, :], "tokT_psum", "tokT", "logits")
                    act.wait_ge(S["logit_shift"], m.i + 1)
                    act.activation(pr[:, :, :], pr[:, :, :], ACT.Exp).then_inc(S["logit_exp"], 1)

            group_bodies(act, body, 1, 5)

        @block.tensor
        def _(pe):
            pe.wait_ge(s_c, 16 * NSMALL)
            for cc in range(KC):
                t = pe.transpose(pl[:, cc * NE:(cc + 1) * NE], wr[:, cc * 128:(cc + 1) * 128], c.ident[0:NE, 0:NE])
            t.then_inc(S["wrT_psum"], 1)
            pe.wait_ge(s_w, 16 * 2)
            pe.wait_ge(S["wrT"], 1)
            pe.wait_ge(S["set"], 6)

            def turn(dst, src, made):
                for cc in range(KC):
                    for t in range(2):
                        x = pe.transpose(dst[:, (cc * 2 + t) * P:(cc * 2 + t + 1) * P],
                                         src[:, t, cc * 128:(cc + 1) * 128], c.ident[0:P, 0:P])
                x.then_inc(S[made], 1)

            def ranks(g):
                pe.wait_ge(S["hits"], g.i + 1)
                wait(pe, S["place"], g.i)
                o = [pk[0:P, k * NE:(k + 1) * NE] for k in range(3)]
                pe.matmul(o[0], earlier[:, :], hits[:, 0, :], start=True, stop=True)
                pe.matmul(o[1], ones[:, :], hits[:, 0, :], start=True, stop=False)
                pe.matmul(o[1], earlier[:, :], hits[:, 1, :], start=False, stop=True)
                pe.matmul(o[2], ones[:, :], hits[:, 0, :], start=True, stop=False)
                pe.matmul(o[2], ones[:, :], hits[:, 1, :], start=False, stop=True).then_inc(S["ranked"], 1)

            def down(t, blocks):
                for f in blocks:
                    x = pe.matmul(pffn[0:P, t * D:(t + 1) * D], fT[:, f, t * P:(t + 1) * P], W2[:, f, :],
                                  start=f == 0, stop=f == NF - 1)
                return x

            def body(g):
                here, prv, old = g.within(0, NGR), g.within(1, NGR + 1), g.within(2, NGR + 2)
                m = g.plus(-1)
                if here:
                    pe.wait_ge(s_qm[g.b], 16 * g.turn + 16)
                    wait(pe, S["tokT"], g.i - 1)
                    turn(pT[0], qm[:, g.b, :, :], "qT_psum")
                    pe.wait_ge(S["h"], g.i + 1)
                    turn(pT[1], h[:, g.b, :, :], "hT_psum")
                    pe.wait_ge(S["qT"], g.i + 1)
                    wait(pe, S["mixn"], g.i)
                    for t in range(2):
                        for cc in range(KC):
                            x = pe.matmul(pmix[0:P, t * D:(t + 1) * D], qT[:, cc, t * P:(t + 1) * P], c.mixmat[:, cc, :],
                                          start=cc == 0, stop=cc == KC - 1)
                    x.then_inc(S["mixed"], 1)
                if here:
                    pe.wait_ge(S["hT"], g.i + 1)
                    for f in range(NF):
                        wait(pe, S["gelu"], g.i * NF + f - 1)
                        for cc in range(KC):
                            x = pe.matmul(ph[f % 2][:, 0:2 * P], W1[:, cc, f * 128:(f + 1) * 128], hT[:, cc, :],
                                          start=cc == 0, stop=cc == KC - 1)
                        x.then_inc(S["hidden"], 1)
                if old:
                    ranks(g.plus(-2))
                if here:
                    pe.wait_ge(S["gelu"], (g.i + 1) * NF)
                    wait(pe, S["r2"], g.i)
                    down(0, range(NF))
                if prv:
                    pe.wait_ge(S["tok"], m.i + 1)
                    turn(pT[0], tok[:, m.b, :, :], "tokT_psum")
                if here:
                    down(1, range(NF // 2))
                if prv:
                    pe.wait_ge(S["tokT"], m.i + 1)
                    for t in range(2):
                        for cc in range(KC):
                            x = pe.matmul(pl[0:P, t * NE:(t + 1) * NE], tokT[:, cc, t * P:(t + 1) * P],
                                          wrT[:, cc, :], start=cc == 0, stop=cc == KC - 1)
                    x.then_inc(S["logits"], 1)
                if here:
                    down(1, range(NF // 2, NF)).then_inc(S["ffn"], 1)

            group_bodies(pe, body, 2, 5)


class Tile:

    def __init__(self, k, off):
        self.k, self.off, self.i = k, off, 4 * k + off

    def plus(self, n):
        return Tile(self.k, self.off + n)

    def place(self, ring):
        return self.off % ring

    def turn(self, ring):
        return 4 // ring * self.k + self.off // ring

    def within(self, low, high):
        return not isinstance(self.i, int) or low <= self.i < high


def tile_bodies(eng, body, extra=0):
    for i in range(4):
        body(Tile(0, i))
    with eng.Fori(1, ETILES // 4 - 1) as k:
        for u in range(4):
            body(Tile(k, u))
    for i in range(4 + extra):
        body(Tile(ETILES // 4 - 1, i))


def expert_phase(nc, c, xp):
    with ExitStack() as ctx:
        def sb(name, shape, dt=F32):
            return ctx.enter_context(nc.sbuf_tensor("m_" + name, shape, dt))

        def sem(name):
            return ctx.enter_context(nc.semaphore("m_" + name))

        reach = sb("reach", [P, NE, NT])
        more = sb("more", [P, NE, NT])
        left = sb("left", [P, NE])
        tiles = sb("tiles", [P, NE])
        ends = sb("ends", [P, NE])
        zero = sb("zero", [P, NE])
        moved = sb("moved", [P, NE])
        chosen = sb("chosen", [P, NGR * 4, NE])
        shift = sb("shift", [P, NGR * 4])
        number = sb("number", [1, ETILES])
        past = sb("past", [1, ETILES, NE])
        skipped = sb("skipped", [1, ETILES, NE])
        which = sb("which", [1, ETILES])
        start = sb("start", [1, ETILES])
        before = sb("before", [1, ETILES])
        whichi, rowi, tail = sb("whichi", [1, ETILES], I32), sb("rowi", [1, ETILES], I32), sb("tail", [1, NE], I32)
        tk = sb("tk", [P, 4, D])
        tkT = sb("tkT", [128, 2, KC, P])
        hid = sb("hid", [P, 2, D])
        hidT = sb("hidT", [128, 2, KC, P])
        y = sb("y", [P, 2, D])
        pt, pu, pt2, py = ([ctx.enter_context(nc.psum_tensor(f"m_{n}{b}", [128, 512], F32)) for b in range(2)]
                           for n in ("pt", "pu", "pt2", "py"))
        s_in = [sem(f"tokens_in{b}") for b in range(4)]
        s_out = [sem(f"y_out{b}") for b in range(2)]
        names = ("iota", "link", "tails", "tables", "zeroed", "tkT_psum", "tkT", "up", "biased", "gelu", "hidT_psum", "hidT",
                 "down", "y", "go")
        S = {n: sem(n) for n in names}
        block = ctx.enter_context(nc.Block())

        def zero_tails(eng, experts):
            eng.wait_ge(S["tails"], 1)
            for e in experts:
                row = eng.value_load(tail[0:1, e:e + 1], min_val=e * CAP, max_val=e * CAP + N)
                eng.dma_start(xp.tok_d[ds(row, P), :], xp.zeros[:, :]).then_inc(S["zeroed"], 16)

        @block.gpsimd
        def _(pool):
            pool.iota(reach[:, :, :], pattern=[[0, NE], [P, NT]], base=0, channel_multiplier=0,
                      allow_small_or_imprecise_dtypes=True).then_inc(S["iota"], 1)
            pool.iota(number[:, :], pattern=[[1, ETILES]], base=0, channel_multiplier=0,
                      allow_small_or_imprecise_dtypes=True).then_inc(S["iota"], 1)

            def body(t):
                pool.wait_ge(S["y"], t.i + 1)
                pool.sem_inc(S["go"], 1)
                pool.dma_start(xp.y_d[ds(t.i * P, P), :], y[:, t.place(2), :]).then_inc(s_out[t.place(2)], 16)

            tile_bodies(pool, body)
            for b in range(2):
                pool.wait_ge(s_out[b], 16 * (ETILES // 2))

        @block.sync
        def _(sp):
            for k in range(SPARE):
                sp.dma_start(xp.tok_d[NE * CAP + k * P:NE * CAP + (k + 1) * P, :], xp.zeros[:, :]).then_inc(S["zeroed"], 16)
            zero_tails(sp, range(NE // 2))
            sp.wait_ge(S["zeroed"], 16 * (SPARE + NE))
            sp.wait_ge(S["tables"], 1)

            def load(t):
                row = sp.value_load(rowi[0:1, ds(t.i, 1)], min_val=0, max_val=NE * CAP + (SPARE - 1) * P)
                wait(sp, S["tkT_psum"], t.i - 3)
                sp.dma_start(tk[:, t.place(4), :], xp.tok_d[ds(row, P), :]).then_inc(s_in[t.place(4)], 16)

            for i in range(3):
                load(Tile(0, i))

            def body(t):
                if t.within(0, ETILES - 3):
                    load(t.plus(3))

            tile_bodies(sp, body)

        @block.vector
        def _(dve):
            cnt = Count(dve, S["link"])
            cnt.mark(dve.memset(zero[:, :], 0.0))
            dve.tensor_copy(tail[:, :], xp.placed[0:1, :]).then_inc(S["tails"], 1)
            cnt.chain(dve.tensor_tensor(left[:, :], xp.placed[:, :], xp.part[:, :], ALU.subtract))
            dve.wait_ge(S["iota"], 2)
            cnt.chain(dve.tensor_tensor(more[:, :, :], left[:, :].unsqueeze(2).broadcast_to([P, NE, NT]),
                                        reach[:, :, :], ALU.is_gt))
            cnt.chain(dve.tensor_reduce(tiles[:, :], more[:, :, :], AX, ALU.add))
            cnt.chain(dve.tensor_tensor_scan(ends[:, :], tiles[:, :], zero[:, :], 0.0, ALU.add, ALU.max))
            cnt.chain(dve.tensor_tensor(past[:, :, :], number[:, :].unsqueeze(2).broadcast_to([1, ETILES, NE]),
                                        ends[0:1, :].unsqueeze(1).broadcast_to([1, ETILES, NE]), ALU.is_ge))
            cnt.mark(dve.tensor_reduce(which[:, :], past[:, :, :], AX, ALU.add))
            cnt.chain(dve.tensor_tensor(skipped[:, :, :], past[:, :, :],
                                        tiles[0:1, :].unsqueeze(1).broadcast_to([1, ETILES, NE]), ALU.mult))
            cnt.chain(dve.tensor_reduce(before[:, :], skipped[:, :, :], AX, ALU.add))
            cnt.chain(dve.tensor_tensor(before[:, :], number[:, :], before[:, :], ALU.subtract))
            cnt.chain(dve.tensor_scalar(start[:, :], which[:, :], float(CAP), None, ALU.mult))
            cnt.chain(dve.scalar_tensor_tensor(start[:, :], before[:, :], float(P), start[:, :], ALU.mult, ALU.add))
            cnt.mark(dve.tensor_copy(rowi[:, :], start[:, :]))
            cnt.chain(dve.tensor_scalar(which[:, :], which[:, :], float(NE - 1), None, ALU.min))
            dve.tensor_copy(whichi[:, :], which[:, :]).then_inc(S["tables"], 1)
            cnt.chain(dve.tensor_tensor(moved[:, :], ends[:, :], tiles[:, :], ALU.subtract))
            cnt.chain(dve.scalar_tensor_tensor(moved[:, :], moved[:, :], float(P), xp.part[:, :],
                                               ALU.mult, ALU.subtract))
            cnt.chain(dve.tensor_tensor(
                chosen[:, :, :], xp.choice[:, :, :, :].rearrange("p g k t -> p (g k t)").unsqueeze(2).broadcast_to([P, NGR * 4, NE]),
                c.iota[0:P, 0:NE].unsqueeze(1).broadcast_to([P, NGR * 4, NE]), ALU.is_equal))
            cnt.chain(dve.tensor_tensor(chosen[:, :, :], chosen[:, :, :],
                                        moved[:, :].unsqueeze(1).broadcast_to([P, NGR * 4, NE]), ALU.mult))
            cnt.chain(dve.tensor_reduce(shift[:, :], chosen[:, :, :], AX, ALU.add))
            dve.tensor_tensor(xp.result[:, :, :].rearrange("p g k -> p (g k)"), shift[:, :],
                              xp.place[:, :, :, :].rearrange("p g k t -> p (g k t)"), ALU.add)
            dve.wait_ge(S["tables"], 1)
            dve.wait_ge(xp.loaded, 16 * 4 * NE)

            def bias_up(t, e):
                dve.wait_ge(S["up"], t.i + 1)
                wait(dve, S["hidT_psum"], t.i - 1)
                dve.tensor_tensor(hid[:, t.place(2), :], pu[t.place(2)][0:P, 0:D],
                                  xp.be[:, 0, ds(e, 1), :].rearrange("p a d -> p (a d)"), ALU.add).then_inc(S["biased"], 1)

            def keep_hidT(t):
                dve.wait_ge(S["hidT_psum"], t.i + 1)
                wait(dve, S["down"], t.i - 1)
                dve.tensor_copy(hidT[:, t.place(2), :, :],
                                pt2[t.place(2)][:, 0:2 * P].rearrange("p (c n) -> p c n", c=KC)).then_inc(S["hidT"], 1)

            def bias_down(t, e):
                dve.wait_ge(S["down"], t.i + 1)
                if t.within(2, ETILES):
                    dve.wait_ge(s_out[t.place(2)], 16 * t.turn(2))
                dve.tensor_tensor(y[:, t.place(2), :], py[t.place(2)][0:P, 0:D],
                                  xp.be[:, 1, ds(e, 1), :].rearrange("p a d -> p (a d)"), ALU.add).then_inc(S["y"], 1)

            def expert_of(t):
                return dve.value_load(whichi[0:1, ds(t.i, 1)], min_val=0, max_val=NE - 1)

            def body(t):
                if t.within(0, ETILES):
                    bias_up(t, expert_of(t))
                if t.within(1, ETILES + 1):
                    keep_hidT(t.plus(-1))
                if t.within(2, ETILES + 2):
                    bias_down(t.plus(-2), expert_of(t.plus(-2)))

            tile_bodies(dve, body, 2)

        @block.scalar
        def _(act):
            zero_tails(act, range(NE // 2, NE))
            act.wait_ge(xp.loaded, 16 * 4 * NE)

            def body(t):
                if t.within(0, ETILES):
                    act.wait_ge(S["tkT_psum"], t.i + 1)
                    wait(act, S["up"], t.i - 1)
                    act.activation(tkT[:, t.place(2), :, :],
                                   pt[t.place(2)][:, 0:2 * P].rearrange("p (c n) -> p c n", c=KC),
                                   ACT.Copy).then_inc(S["tkT"], 1)
                if t.within(1, ETILES + 1):
                    b = t.plus(-1).place(2)
                    act.wait_ge(S["biased"], t.i)
                    act.activation(hid[:, b, :], hid[:, b, :], ACT.Gelu).then_inc(S["gelu"], 1)

            tile_bodies(act, body, 1)

        @block.tensor
        def _(pe):
            pe.wait_ge(xp.loaded, 16 * 4 * NE)
            pe.wait_ge(S["tables"], 1)

            def turn(t):
                pe.wait_ge(s_in[t.place(4)], 16 * t.turn(4) + 16)
                wait(pe, S["tkT"], t.i - 1)
                for cc in range(KC):
                    x = pe.transpose(pt[t.place(2)][:, cc * P:(cc + 1) * P], tk[:, t.place(4), cc * 128:(cc + 1) * 128],
                                     c.ident[0:P, 0:P])
                x.then_inc(S["tkT_psum"], 1)

            def turn_hidden(t):
                b = t.place(2)
                pe.wait_ge(S["gelu"], t.i + 1)
                wait(pe, S["hidT"], t.i - 1)
                for cc in range(KC):
                    x = pe.transpose(pt2[b][:, cc * P:(cc + 1) * P], hid[:, b, cc * 128:(cc + 1) * 128],
                                     c.ident[0:P, 0:P])
                x.then_inc(S["hidT_psum"], 1)

            def expert_of(t):
                return pe.value_load(whichi[0:1, ds(t.i, 1)], min_val=0, max_val=NE - 1)

            def product(out, lhsT, weights, e, done):
                for cc in range(KC):
                    x = pe.matmul(out, lhsT[:, cc, :], weights[:, ds(e, 1), cc, :].rearrange("p a d -> p (a d)"),
                                  start=cc == 0, stop=cc == KC - 1)
                x.then_inc(done, 1)

            def body(t):
                m = t.plus(-2)
                if t.within(0, ETILES):
                    up = expert_of(t)
                    known[t.off] = up
                if t.within(2, ETILES + 2):
                    down = known[m.off] if not isinstance(m.k, int) and m.off >= 0 else expert_of(m)
                if t.within(0, ETILES - 1):
                    turn(t.plus(1))
                if t.within(0, ETILES):
                    pe.wait_ge(S["tkT"], t.i + 1)
                    wait(pe, S["biased"], t.i - 1)
                    product(pu[t.place(2)][0:P, 0:D], tkT[:, t.place(2), :, :], xp.We1, up, S["up"])
                if t.within(1, ETILES + 1):
                    turn_hidden(t.plus(-1))
                if t.within(2, ETILES + 2):
                    pe.wait_ge(S["hidT"], m.i + 1)
                    wait(pe, S["y"], m.i - 1)
                    product(py[m.place(2)][0:P, 0:D], hidT[:, m.place(2), :, :], xp.We2, down, S["down"])

            known = {}
            turn(Tile(0, 0))
            tile_bodies(pe, body, 2)


def combine_phase(nc, c, xp, out):
    with ExitStack() as ctx:
        def sb(name, shape, dt=F32):
            return ctx.enter_context(nc.sbuf_tensor("f_" + name, shape, dt))

        def sem(name):
            return ctx.enter_context(nc.semaphore("f_" + name))

        idx = sb("idx", [P, 2, 4], I32)
        ya = sb("ya", [P, 2, 4, D])
        acc = sb("acc", [P, 2, 2, D])
        s_ya, s_in, s_out = ([sem(f"{n}{b}") for b in range(2)] for n in ("y_in", "base_in", "out"))
        s_idx, s_go, s_one, s_sum = sem("idx"), sem("go"), sem("first_added"), sem("both_added")
        block = ctx.enter_context(nc.Block())

        @block.gpsimd
        def _(pool):
            def body(g):
                wait(pool, s_sum, g.i - 1)
                pool.tensor_copy(idx[:, g.b, :], xp.result[:, ds(g.i, 1), :].rearrange("p a k -> p (a k)")
                                 ).then_inc(s_idx, 1)
                pool.wait_ge(s_idx, g.i + 1)
                pool.sem_inc(s_go, 1)
                for k in range(4):
                    pool.indirect_dma_start(out=ya[:, g.b, k, :], out_offset=None, in_=xp.y_d[:, :],
                                            in_offset=bass.IndirectOffsetOnAxis(ap=idx[:, g.b, k:k + 1], axis=0)
                                            ).then_inc(s_ya[g.b], 16)

            group_bodies(pool, body)

        @block.vector
        def _(dve):
            def body(g):
                dve.wait_ge(s_ya[g.b], 64 * g.turn + 64)
                dve.wait_ge(s_in[g.b], 16 * g.turn + 16)
                for k in range(2):
                    for t in range(2):
                        m = dve.scalar_tensor_tensor(
                            acc[:, g.b, t, :], ya[:, g.b, 2 * k + t, :],
                            xp.share[:, ds(g.i, 1), k, t], acc[:, g.b, t, :], ALU.mult, ALU.add)
                    m.then_inc(s_sum if k else s_one, 1)
                    if k == 0:
                        dve.wait_ge(s_one, g.i + 1)

            group_bodies(dve, body)

        @block.sync
        def _(sp):
            def rows(d, g):
                return d[ds(g.i * (2 * P), 2 * P), :].rearrange("(t p) d -> p t d", p=P)

            def load(g):
                if g.within(2, NGR):
                    sp.wait_ge(s_out[g.b], 16 * g.turn)
                sp.dma_start(acc[:, g.b, :, :], rows(xp.base_d, g)).then_inc(s_in[g.b], 16)

            load(Group(0, 0))

            def body(g):
                if g.within(0, NGR - 1):
                    load(g.plus(1))
                sp.wait_ge(s_sum, g.i + 1)
                sp.dma_start(rows(out, g), acc[:, g.b, :, :]).then_inc(s_out[g.b], 16)

            group_bodies(sp, body)
            for b in range(2):
                sp.wait_ge(s_out[b], 16 * ((NGR + 1 - b) // 2))


_INS = ['x', 'src', 'dst', 'L0_gnn_Wq', 'L0_gnn_bq', 'L0_gnn_Wk', 'L0_gnn_bk', 'L0_gnn_Wv', 'L0_gnn_bv',
        'L0_gnn_Wskip', 'L0_gnn_bskip', 'L0_gnn_ln1_g', 'L0_gnn_ln1_b', 'L0_gnn_W1', 'L0_gnn_b1', 'L0_gnn_W2',
        'L0_gnn_b2', 'L0_gnn_ln2_g', 'L0_gnn_ln2_b', 'L0_mix_Wqkv', 'L0_mix_Wout', 'L0_mix_gamma',
        'L0_ffn_router_w', 'L0_ffn_w1', 'L0_ffn_b1', 'L0_ffn_w2', 'L0_ffn_b2']


def build(nc, w, out):
    kv_d = nc.dram_tensor("kv_rows", (N, ROW), F32, kind="Internal").ap()
    s1_d = nc.dram_tensor("skip_rows", (N, D), F32, kind="Internal").ap()
    qm_d = nc.dram_tensor("mixq_rows", (N, D), F32, kind="Internal").ap()
    with ExitStack() as ctx:
        c = Consts(ctx, nc)
        used = []
        constants(nc, c, used)
        node_phase(nc, c, used, w["x"], w, kv_d, s1_d, qm_d)
        nc.clear_and_free_semaphores(used)
        nc.all_engine_barrier()
        with ExitStack() as ectx:
            st = Steps(ectx, nc)
            step_tables(nc, c, st, w["src"], w["dst"])
            edge_phase(nc, c, st, kv_d)
        xp = Routed(ctx, nc)
        dense_phase(nc, c, xp, w, s1_d, qm_d)
        expert_phase(nc, c, xp)
        combine_phase(nc, c, xp, out)


def kernel(**inputs):
    import numpy as _np
    import concourse.bacc as _bacc
    from concourse import mybir as _mybir
    from concourse.bass_utils import run_bass_kernel_spmd as _run

    nc = _bacc.Bacc("TRN2", target_bir_lowering=False, num_devices=1)
    arrays, args = {}, {}
    for name in _INS:
        a = _np.ascontiguousarray(inputs[name])
        arrays[f"in_{name}_dram"] = a
        args[name] = nc.dram_tensor(f"in_{name}_dram", a.shape, _mybir.dt.from_np(a.dtype), kind="ExternalInput").ap()
    out = nc.dram_tensor("out_dram", (N, D), _mybir.dt.float32, kind="ExternalOutput").ap()
    build(nc, args, out)
    r = _run(nc, [arrays], core_ids=[0])
    return r.results[0]["out_dram"]
```
